# Optimizing a Trainium2 kernel written in Bass

```python
import numpy as np
import jax
import jax.numpy as jnp

def _softmax(x, axis=-1):
    return jax.nn.softmax(x, axis=axis)

def _gelu(x):
    return jax.nn.gelu(x, approximate=True)

def _silu(x):
    return jax.nn.silu(x)

def _sigmoid(x):
    return jax.nn.sigmoid(x)

def _layernorm(x, axis=-1, eps=1e-05):
    m = jnp.mean(x, axis=axis, keepdims=True)
    v = jnp.var(x, axis=axis, keepdims=True)
    return (x - m) / jnp.sqrt(v + eps)

def _scatter_add(tgt, idx, src, axis=0):
    return tgt.at[idx].add(src)

def _segment_sum(src, seg, n):
    return jax.ops.segment_sum(src, seg, n)
kernel_name = 'mk_prb_d1_jaxref_r4_1b933d'

def setup_inputs(seed: int=0):
    np.random.seed(seed)
    _w = jnp.asarray

    def _L0_attn_setup():
        import jax, jax.numpy as jnp
        import numpy as np
        EMBED_DIM = 256
        NUM_HEADS = 16
        NUM_GLOBAL = 4
        NUM_LOCAL = NUM_HEADS - NUM_GLOBAL
        WINDOW = 64
        HEAD_DIM = EMBED_DIM // NUM_HEADS

        def _masks(seq_len):
            i = jnp.arange(seq_len)[:, None]
            j = jnp.arange(seq_len)[None, :]
            diff = i - j
            global_mask = diff < 0
            local_mask = (diff < 0) | (diff > WINDOW)
            return (global_mask, local_mask)

        def _attend(q, k, v, mask):
            scores = jnp.einsum('bhqd,bhkd->bhqk', q, k) * HEAD_DIM ** (-0.5)
            scores = jnp.where(mask[None, None], -jnp.inf, scores)
            w = jax.nn.softmax(scores, axis=-1)
            return jnp.einsum('bhqk,bhkd->bhqd', w, v)
        key = jax.random.key(seed)
        k1, k2, k3 = jax.random.split(key, 3)
        B, S = (4, 512)
        x = jax.random.normal(k1, (B, S, EMBED_DIM), dtype=jnp.float32)
        w_qkv = jax.random.normal(k2, (EMBED_DIM, 3 * EMBED_DIM), dtype=jnp.float32) * EMBED_DIM ** (-0.5)
        b_qkv = jnp.zeros((3 * EMBED_DIM,), dtype=jnp.float32)
        w_out = jax.random.normal(k3, (EMBED_DIM, EMBED_DIM), dtype=jnp.float32) * EMBED_DIM ** (-0.5)
        b_out = jnp.zeros((EMBED_DIM,), dtype=jnp.float32)
        return {'x': x, 'w_qkv': w_qkv, 'b_qkv': b_qkv, 'w_out': w_out, 'b_out': b_out}
    _L0_attn_in = _L0_attn_setup()

    def _L0_ffn_setup():
        import jax, jax.numpy as jnp
        import numpy as np
        B, T, D, R, KEXP = (4, 1024, 256, 64, 8)
        RH = max(D, 32)
        SCALE = 0.02

        def _fused_branch(Q_side, K_side, V, W, U, b, router_w1, router_b1, router_w2, router_b2, expert_bias):
            xV = jnp.einsum('btd,kdr->btkr', Q_side, V)
            yW = jnp.einsum('btd,kdr->btkr', K_side, W)
            cum_yW = jnp.cumsum(yW, axis=1)
            prod = xV * cum_yW
            h = jax.nn.gelu(Q_side @ router_w1.T + router_b1, approximate=False)
            logits = h @ router_w2.T + router_b2 + expert_bias
            weights = jax.nn.softmax(logits, axis=-1)
            out = jnp.einsum('btkr,kdr->btd', prod * weights[..., None], U)
            out = out + weights @ b
            n_valid = jnp.arange(1, Q_side.shape[1] + 1, dtype=Q_side.dtype)
            return out / n_valid[None, :, None]
        key = jax.random.key(seed)
        ks = jax.random.split(key, 20)
        x = jax.random.normal(ks[0], (B, T, D), dtype=jnp.float32)
        W_Q = jax.random.normal(ks[1], (D, D), dtype=jnp.float32) * (1.0 / np.sqrt(D))
        W_K = jax.random.normal(ks[2], (D, D), dtype=jnp.float32) * (1.0 / np.sqrt(D))
        W_O = jax.random.normal(ks[3], (D, D), dtype=jnp.float32) * (1.0 / np.sqrt(D))
        W_inv = jnp.eye(D, dtype=jnp.float32) + 0.01 * jax.random.normal(ks[4], (D, D), dtype=jnp.float32)
        V_fwd = jax.random.normal(ks[5], (KEXP, D, R), dtype=jnp.float32) * SCALE
        W_fwd = jax.random.normal(ks[6], (KEXP, D, R), dtype=jnp.float32) * SCALE
        U_fwd = jax.random.normal(ks[7], (KEXP, D, R), dtype=jnp.float32) * SCALE
        b_fwd = jnp.zeros((KEXP, D), dtype=jnp.float32)
        V_inv = jax.random.normal(ks[8], (KEXP, D, R), dtype=jnp.float32) * SCALE
        W_inv_exp = jax.random.normal(ks[9], (KEXP, D, R), dtype=jnp.float32) * SCALE
        U_inv = jax.random.normal(ks[10], (KEXP, D, R), dtype=jnp.float32) * SCALE
        b_inv = jnp.zeros((KEXP, D), dtype=jnp.float32)
        router_w1 = jax.random.normal(ks[11], (RH, D), dtype=jnp.float32) * (1.0 / np.sqrt(D))
        router_b1 = jnp.zeros((RH,), dtype=jnp.float32)
        router_w2 = jax.random.normal(ks[12], (KEXP, RH), dtype=jnp.float32) * (1.0 / np.sqrt(RH))
        router_b2 = jnp.zeros((KEXP,), dtype=jnp.float32)
        alpha_bi = jnp.asarray(0.5, dtype=jnp.float32)
        expert_bias = jnp.zeros((KEXP,), dtype=jnp.float32)
        return dict(x=x, W_Q=W_Q, W_K=W_K, W_O=W_O, W_inv=W_inv, V_fwd=V_fwd, W_fwd=W_fwd, U_fwd=U_fwd, b_fwd=b_fwd, V_inv=V_inv, W_inv_exp=W_inv_exp, U_inv=U_inv, b_inv=b_inv, router_w1=router_w1, router_b1=router_b1, router_w2=router_w2, router_b2=router_b2, alpha_bi=alpha_bi, expert_bias=expert_bias)
    _L0_ffn_in = _L0_ffn_setup()
    _d = {'L0_attn_x': _L0_attn_in['x'], 'L0_attn_w_qkv': _L0_attn_in['w_qkv'], 'L0_attn_b_qkv': _L0_attn_in['b_qkv'], 'L0_attn_w_out': _L0_attn_in['w_out'], 'L0_attn_b_out': _L0_attn_in['b_out'], 'L0_ffn_W_Q': _L0_ffn_in['W_Q'], 'L0_ffn_W_K': _L0_ffn_in['W_K'], 'L0_ffn_W_O': _L0_ffn_in['W_O'], 'L0_ffn_W_inv': _L0_ffn_in['W_inv'], 'L0_ffn_V_fwd': _L0_ffn_in['V_fwd'], 'L0_ffn_W_fwd': _L0_ffn_in['W_fwd'], 'L0_ffn_U_fwd': _L0_ffn_in['U_fwd'], 'L0_ffn_b_fwd': _L0_ffn_in['b_fwd'], 'L0_ffn_V_inv': _L0_ffn_in['V_inv'], 'L0_ffn_W_inv_exp': _L0_ffn_in['W_inv_exp'], 'L0_ffn_U_inv': _L0_ffn_in['U_inv'], 'L0_ffn_b_inv': _L0_ffn_in['b_inv'], 'L0_ffn_router_w1': _L0_ffn_in['router_w1'], 'L0_ffn_router_b1': _L0_ffn_in['router_b1'], 'L0_ffn_router_w2': _L0_ffn_in['router_w2'], 'L0_ffn_router_b2': _L0_ffn_in['router_b2'], 'L0_ffn_alpha_bi': _L0_ffn_in['alpha_bi'], 'L0_ffn_expert_bias': _L0_ffn_in['expert_bias']}
    _x0 = _d['L0_attn_x']
    _d['L0_attn_x'] = jax.random.normal(jax.random.fold_in(jax.random.key(seed), 1), (8, 1024, 256), dtype=_x0.dtype)
    del _x0
    return _d

def reference(L0_attn_x, L0_attn_w_qkv, L0_attn_b_qkv, L0_attn_w_out, L0_attn_b_out, L0_ffn_W_Q, L0_ffn_W_K, L0_ffn_W_O, L0_ffn_W_inv, L0_ffn_V_fwd, L0_ffn_W_fwd, L0_ffn_U_fwd, L0_ffn_b_fwd, L0_ffn_V_inv, L0_ffn_W_inv_exp, L0_ffn_U_inv, L0_ffn_b_inv, L0_ffn_router_w1, L0_ffn_router_b1, L0_ffn_router_w2, L0_ffn_router_b2, L0_ffn_alpha_bi, L0_ffn_expert_bias):

    def _L0_attn_ref(x, w_qkv, b_qkv, w_out, b_out):
        import jax, jax.numpy as jnp
        import numpy as np
        EMBED_DIM = 256
        NUM_HEADS = 16
        NUM_GLOBAL = 4
        NUM_LOCAL = NUM_HEADS - NUM_GLOBAL
        WINDOW = 64
        HEAD_DIM = EMBED_DIM // NUM_HEADS

        def _masks(seq_len):
            i = jnp.arange(seq_len)[:, None]
            j = jnp.arange(seq_len)[None, :]
            diff = i - j
            global_mask = diff < 0
            local_mask = (diff < 0) | (diff > WINDOW)
            return (global_mask, local_mask)

        def _attend(q, k, v, mask):
            scores = jnp.einsum('bhqd,bhkd->bhqk', q, k) * HEAD_DIM ** (-0.5)
            scores = jnp.where(mask[None, None], -jnp.inf, scores)
            w = jax.nn.softmax(scores, axis=-1)
            return jnp.einsum('bhqk,bhkd->bhqd', w, v)
        B, S, _ = x.shape
        qkv = x @ w_qkv + b_qkv
        q, k, v = jnp.split(qkv, 3, axis=-1)

        def heads(t):
            return t.reshape(B, S, NUM_HEADS, HEAD_DIM).transpose(0, 2, 1, 3)
        q, k, v = (heads(q), heads(k), heads(v))
        gmask, lmask = _masks(S)
        ctx_g = _attend(q[:, :NUM_GLOBAL], k[:, :NUM_GLOBAL], v[:, :NUM_GLOBAL], gmask)
        ctx_l = _attend(q[:, NUM_GLOBAL:], k[:, NUM_GLOBAL:], v[:, NUM_GLOBAL:], lmask)
        ctx = jnp.concatenate([ctx_g, ctx_l], axis=1)
        ctx = ctx.transpose(0, 2, 1, 3).reshape(B, S, EMBED_DIM)
        return ctx @ w_out + b_out

    def _L0_ffn_ref(x, W_Q, W_K, W_O, W_inv, V_fwd, W_fwd, U_fwd, b_fwd, V_inv, W_inv_exp, U_inv, b_inv, router_w1, router_b1, router_w2, router_b2, alpha_bi, expert_bias):
        import jax, jax.numpy as jnp
        import numpy as np
        B, T, D, R, KEXP = (4, 1024, 256, 64, 8)
        RH = max(D, 32)
        SCALE = 0.02

        def _fused_branch(Q_side, K_side, V, W, U, b, router_w1, router_b1, router_w2, router_b2, expert_bias):
            xV = jnp.einsum('btd,kdr->btkr', Q_side, V)
            yW = jnp.einsum('btd,kdr->btkr', K_side, W)
            cum_yW = jnp.cumsum(yW, axis=1)
            prod = xV * cum_yW
            h = jax.nn.gelu(Q_side @ router_w1.T + router_b1, approximate=False)
            logits = h @ router_w2.T + router_b2 + expert_bias
            weights = jax.nn.softmax(logits, axis=-1)
            out = jnp.einsum('btkr,kdr->btd', prod * weights[..., None], U)
            out = out + weights @ b
            n_valid = jnp.arange(1, Q_side.shape[1] + 1, dtype=Q_side.dtype)
            return out / n_valid[None, :, None]
        Q = x @ W_Q.T
        K = x @ W_K.T
        invQ = Q @ W_inv.T
        invK = K @ W_inv.T
        fwd = _fused_branch(Q, K, V_fwd, W_fwd, U_fwd, b_fwd, router_w1, router_b1, router_w2, router_b2, expert_bias)
        inv = _fused_branch(invQ, invK, W_inv_exp, V_inv, U_inv, b_inv, router_w1, router_b1, router_w2, router_b2, expert_bias)
        out = fwd + alpha_bi * inv
        return out @ W_O.T
    x = L0_attn_x
    xn = _layernorm(x, axis=-1)
    x = x + _L0_attn_ref(xn, L0_attn_w_qkv, L0_attn_b_qkv, L0_attn_w_out, L0_attn_b_out) + _L0_ffn_ref(xn, L0_ffn_W_Q, L0_ffn_W_K, L0_ffn_W_O, L0_ffn_W_inv, L0_ffn_V_fwd, L0_ffn_W_fwd, L0_ffn_U_fwd, L0_ffn_b_fwd, L0_ffn_V_inv, L0_ffn_W_inv_exp, L0_ffn_U_inv, L0_ffn_b_inv, L0_ffn_router_w1, L0_ffn_router_b1, L0_ffn_router_w2, L0_ffn_router_b2, L0_ffn_alpha_bi, L0_ffn_expert_bias)
    return x

_drawn_inputs = setup_inputs


def setup_inputs(seed=0):
    import zlib

    import numpy as np

    out = dict(_drawn_inputs(seed))
    spreads = {'L0_attn_b_qkv': (0.0, 0.1),
     'L0_attn_b_out': (0.0, 0.1),
     'L0_ffn_b_fwd': (0.0, 0.1),
     'L0_ffn_b_inv': (0.0, 0.1),
     'L0_ffn_router_b1': (0.0, 0.1),
     'L0_ffn_router_b2': (0.0, 0.1),
     'L0_ffn_expert_bias': (0.0, 0.1)}
    factors = {}
    for name, (base, spread) in spreads.items():
        noise = np.random.default_rng([zlib.crc32(name.encode()), seed]).standard_normal(out[name].shape)
        drawn = base * np.exp(spread * noise) if base else spread * noise
        out[name] = jnp.asarray(drawn.astype(out[name].dtype))
    for name, factor in factors.items():
        out[name] = (out[name] * factor).astype(out[name].dtype)
    return out
```

```python
from contextlib import ExitStack

import concourse.bass as bass
from concourse import mybir

F32 = mybir.dt.float32
F32R = mybir.dt.float32r
BF16 = mybir.dt.bfloat16
I32 = mybir.dt.int32
ALU = mybir.AluOpType
ACT = mybir.ActivationFunctionType
AX_X = mybir.AxisListType.X

P = 128
WINDOW = 64
N_GLOBAL = 4
LN_EPS = 1e-5
MASKED = -1e30
LOWEST = -3e38


class Tally:

    def __init__(self, sem):
        self.sem = sem
        self.n = 0


class Mark:

    def __init__(self, tally, value):
        self.tally, self.value = tally, value


class Slot:

    def __init__(self, name):
        self.name, self.free = name, []


class Queue:

    def __init__(self):
        self.items = []

    def wait(self, *marks):
        for m in marks:
            self.items.append(("wait", m))

    def wait_free(self, slot):
        if slot.free:
            self.wait(*slot.free)
        else:
            self.items.append(("wait_last_turn", slot))

    def do(self, fn, tally=None, by=1, apart=False):
        if apart:
            self.items.append(("do", lambda e, _: e.nop(nofuse=True), None, 0))
        if tally is None:
            self.items.append(("do", fn, None, 0))
            return None
        tally.n += by
        self.items.append(("do", fn, tally, by))
        return Mark(tally, tally.n)

    def write(self, eng, turn=None, waits_apart=False):
        seen = {}
        for item in self.items:
            if item[0] == "wait":
                tally, value = item[1].tally, item[1].value
                if seen.get(tally, -(1 << 30)) >= value:
                    continue
                seen[tally] = value
                eng.wait_ge(tally.sem, value if turn is None else turn * tally.n + (tally.n + value))
                if waits_apart:
                    eng.nop(nofuse=True)
            elif item[0] == "wait_last_turn":
                if turn is None:
                    continue
                for m in item[1].free:
                    tally, value = m.tally, m.value - m.tally.n
                    if seen.get(tally, -(1 << 30)) >= value:
                        continue
                    seen[tally] = value
                    eng.wait_ge(tally.sem, turn * tally.n + m.value)
                    if waits_apart:
                        eng.nop(nofuse=True)
            else:
                _, fn, tally, by = item
                ins = fn(eng, turn)
                if tally is not None:
                    ins.then_inc(tally.sem, by)


def mixer_layer(
    nc, x, w_qkv, b_qkv, w_out, b_out, W_Q, W_K, W_O, W_inv, V_fwd, W_fwd, U_fwd, b_fwd,
    V_inv, W_inv_exp, U_inv, b_inv, router_w1, router_b1, router_w2, router_b2, alpha, expert_bias, out,
):
    NB, S, D = x.shape
    KE, _, R = V_fwd.shape
    HD = 16
    NH = D // HD
    NG = N_GLOBAL
    NL = NH - NG
    KR = KE * R
    DB = D // P
    KB = KR // P
    C = 512
    NC = S // C
    T = C // P
    ST = S // P
    SCALE = float(HD) ** -0.5
    assert DB == 2 and NC == 2 and KR == 512 and NG == 4 and NL % 4 == 0 and C // WINDOW == 8
    COL_Q, COL_K, COL_V = 0, D, 2 * D
    COL_R = 3 * D
    COL_X = COL_R + 2 * D
    COL_C = COL_X + 2 * KR
    NCOL = COL_C + 2 * KR
    G16 = 6 * HD
    KSTK = G16 + 3
    LEFT, RIGHT = (0, 0, 0, 1, 1, 2), (0, 1, 2, 0, 1, 0)
    VW = HD + 1

    ctx = ExitStack()
    with ctx:
        def sb(name, shape, dt=F32):
            return ctx.enter_context(nc.sbuf_tensor(name, shape, dt))

        def tally(name):
            return Tally(ctx.enter_context(nc.semaphore(name)))

        WH = sb("WH", [P, DB, NCOL], F32R)
        WL = sb("WL", [P, DB, NCOL], F32R)
        UH = sb("UH", [P, 2 * KB, D], F32R)
        UL = sb("UL", [P, 2 * KB, D], F32R)
        OH = sb("OH", [P, DB, D], F32R)
        OL = sb("OL", [P, DB, D], F32R)
        bias_rows = sb("bias_rows", [KSTK, D], BF16)
        spread = sb("spread", [KSTK, 2 * KB, P], BF16)
        W2 = sb("W2", [P, 2 * DB, 2 * KE])
        ident = sb("ident", [P, P])
        ident_b = sb("ident_b", [P, P], BF16)
        band = sb("band", [P, 2, P + WINDOW])
        strip = sb("strip", [P, C])
        q_bias = sb("q_bias", [P, DB])
        k_bias = sb("k_bias", [P, DB])
        r_bias = sb("r_bias", [P, DB])
        l_bias = sb("l_bias", [2 * KE, 2])
        inv_n = sb("inv_n", [P, ST])

        QS_W = NH * C // 2
        KL_W = NL * (C + WINDOW) // 2
        KG_W = NG * S // 2
        PT_W = 2 * 3 * DB * C // 2
        X_W = T * D
        AREA = QS_W + KL_W + KG_W + PT_W + 2 * X_W
        area = sb("area", [P, AREA])
        at = [0]

        def carve(width):
            a = area[:, at[0]:at[0] + width]
            at[0] += width
            return a

        QS = carve(QS_W).bitcast(BF16).rearrange("p (h t) -> p h t", h=NH)
        KL = carve(KL_W).bitcast(BF16).rearrange("p (h t) -> p h t", h=NL)
        KG = carve(KG_W).bitcast(BF16).rearrange("p (h t) -> p h t", h=NG)
        parts = carve(PT_W).bitcast(BF16).rearrange("p (w i b t) -> p w i b t", w=2, i=3, b=DB)
        xt = [carve(X_W).rearrange("p (t d) -> p t d", t=T) for _ in range(2)]

        tok = sb("tok", [P, T, D])
        XH = sb("XH", [P, DB, C], F32R)
        XL = sb("XL", [P, DB, C], F32R)
        CH = sb("CH", [P, DB, C], F32R)
        CL = sb("CL", [P, DB, C], F32R)
        rest = sb("rest", [P, 2, C])
        carry = sb("carry", [P, DB])
        stats = sb("stats", [P, T, 6])
        mv = sb("mv", [P, T, 2])
        var = sb("var", [P, 6, T])
        Va = sb("Va", [P, ST, NH, VW])
        Vs = sb("Vs", [P, T, NL, VW])
        HE = sb("HE", [P, 4, C])
        logit_f = sb("logit_f", [2 * KE, C])
        gate = sb("gate", [P, 4, T, 2 * KE])
        gsum = sb("gsum", [P, 4, T * 2])
        wstack = sb("wstack", [P, T, KSTK], BF16)
        WT = sb("WT", [KSTK, C], BF16)
        prod = sb("prod", [P, 3, C])
        PH = sb("PH", [P, 2, C], F32R)
        PL = sb("PL", [P, 2, C], F32R)
        positions = sb("positions", [P, ST], I32)
        peak = sb("peak", [P, T, NH])
        peak_rest = sb("peak_rest", [P, 2, T, NH])
        peak_part = sb("peak_part", [P, T, NG])
        peak_t = sb("peak_t", [P, T, 3 * NH], BF16)
        peak_f = sb("peak_f", [3 * NH, C], BF16)
        craw = sb("craw", [P, 2, C])
        cinv = sb("cinv", [P, 2, T, 4])
        PS = ctx.enter_context(nc.psum_tensor("PS", [P, 8, 512], F32))

        parts_d = nc.dram_tensor("parts_d", (2, 3, D, C), BF16, kind="Internal").ap()
        peak_d = nc.dram_tensor("peak_d", (3 * NH, C), BF16, kind="Internal").ap()

        pe, act, dve, pool, sp = (Queue() for _ in range(5))
        s_raw = tally("raw_loaded")
        s_pe0 = tally("setup_pe")
        s_act0 = tally("setup_act")
        s_dve0 = tally("setup_dve")
        s_pool0 = tally("setup_pool")
        s_put0 = tally("setup_rows_put")
        at[0] = 0
        at_raw = {}

        def raw(name, shape):
            n = 1
            for d in shape:
                n *= d
            a = carve(n)
            at_raw[name] = a.rearrange("p (a b) -> p a b", a=shape[0])
            return at_raw[name]

        rWQ, rWK, rWI, rWO, rR1 = (raw(n, (DB, D)) for n in ("wq", "wk", "wi", "wo", "r1"))
        tWI, tWO, tR1, gQ, gK = (raw(n, (DB, D)) for n in ("twi", "two", "tr1", "gq", "gk"))
        rV = [raw(n, (DB, KR)) for n in ("vf", "vi", "cf", "ci")]
        rU = [raw(n, (DB, KR)) for n in ("uf", "ui")]
        rQKV = raw("qkv", (DB, 3 * D))
        rOUT = raw("out", (DB, D))
        assert at[0] <= AREA
        braw = HE[:, 0, 0:DB * 2 * KE].rearrange("p (w b k) -> p w b k", w=2, b=DB)
        bvraw = HE[:, 1, 0:DB]
        borow = HE[0:1, 2, 0:D]
        alpha1 = HE[0:1, 3, 0:1]
        ones1 = HE[0:1, 3, 8:8 + P]
        alphac = HE[:, 3, 200:201]
        brow = [rest[0:n, i, j:j + D] for n, i, j in ((KE, 0, 0), (KE, 0, D), (1, 1, 0))]
        brest = [[prod[0:n, i, j:j + D] for i in (0, 1)] for n, j in ((KE, 0), (KE, D))] + \
                [[prod[0:1, 2, j:j + D] for j in (0, D)]]
        bpart = [[craw[0:n, j, D * i // 2:D * (i + 1) // 2].bitcast(BF16) for i in range(3)]
                 for n, j in ((KE, 0), (KE, 1))] + \
                [[logit_f[0:1, D * i // 2:D * (i + 1) // 2].bitcast(BF16) for i in range(3)]]

        def load(dst, src):
            return sp.do(lambda e, _: e.dma_start(dst, src), s_raw, 16)

        for dst, src in ((rWQ, W_Q), (rWK, W_K), (rWI, W_inv), (rWO, W_O), (rR1, router_w1), (rOUT, w_out)):
            load(dst, src.rearrange("(b p) d -> p b d", p=P))
        load(rQKV, w_qkv.rearrange("(b p) d -> p b d", p=P))
        for dst, src in zip(rV + rU, (V_fwd, W_inv_exp, W_fwd, V_inv, U_fwd, U_inv)):
            for b in range(DB):
                load(dst[:, b, :].rearrange("p (k r) -> p k r", k=KE), src[:, b * P:(b + 1) * P, :].rearrange("k p r -> p k r"))
        for dst, lo in ((q_bias, 0), (k_bias, D), (bvraw, 2 * D)):
            load(dst[:, :] if dst is not bvraw else bvraw, b_qkv[lo:lo + D].rearrange("(b p) -> p b", p=P))
        load(r_bias[:, :], router_b1.rearrange("(b p) -> p b", p=P))
        for w, src in ((0, b_fwd), (1, b_inv)):
            for b in range(DB):
                load(braw[:, w, b, :], src[:, b * P:(b + 1) * P].rearrange("k p -> p k"))
        load(borow, b_out.rearrange("(a d) -> a d", a=1))
        load(alpha1, alpha.rearrange("(a d) -> a d", a=1))
        for w in range(2):
            load(l_bias[KE * w:KE * (w + 1), 0:1], router_b2.rearrange("(k a) -> k a", a=1))
            load(l_bias[KE * w:KE * (w + 1), 1:2], expert_bias.rearrange("(k a) -> k a", a=1))

        zeroed = dve.do(lambda e, _: e.memset(W2[:, :, :], 0.0), s_dve0)
        sp.wait(zeroed)
        for w in range(2):
            for b in range(DB):
                raw_in = load(W2[:, DB * w + b, KE * w:KE * (w + 1)], router_w2[:, b * P:(b + 1) * P].rearrange("k p -> p k"))

        for view, value in ((ident[:, :], 0.0), (ident_b[:, :], 0.0), (band[:, :, :], 0.0), (strip[:, :], 0.0),
                            (spread[:, :, :], 0.0), (ones1, 1.0), (wstack[:, :, :], 1.0), (Va[:, :, :, :], 1.0),
                            (craw[:, :, :], 0.0), (PS[:, :, :], 0.0)):
            cleared = dve.do(lambda e, _, view=view, value=value: e.memset(view, value), s_dve0)
        pool.wait(cleared)

        def select(view, pattern, base, cm, op=ALU.is_ge, fill=MASKED):
            m = pool.do(lambda e, _: e.affine_select(out=view, in_=view, compare_op=op, fill=fill, base=base,
                                                     pattern=pattern, channel_multiplier=cm), s_pool0)
            pool.wait(m)
            return m

        for view in (ident[:, :], ident_b[:, :]):
            select(view, [[1, P]], 0, -1, ALU.not_equal, 1.0)
        BW = P + WINDOW
        for v in range(2):
            select(band[:, v, :], [[1, BW]], 0, -1)
            select(band[:, v, :], [[-1, BW]], WINDOW, 1)
        select(band[:, 1, :], [[1, BW]], -WINDOW, 0)
        select(strip[:, :], [[-1, C]], C - P, 1)
        for first in (0, 3 * HD, 5 * HD):
            view = spread[:, :, :].rearrange("r j (a m) -> r (j a) m", a=2)
            consts_in = select(view, [[-1, 4 * KB], [0, R]], -first, 1, ALU.not_equal, 1.0)
        count = positions[:, :]
        counted = pool.do(lambda e, _: e.iota(count, pattern=[[P, ST]], base=1, channel_multiplier=1), s_pool0)
        dve.wait(counted)
        dve.wait(dve.do(lambda e, _: e.tensor_copy(inv_n[:, :], count), s_dve0))
        dve.wait(dve.do(lambda e, _: e.reciprocal(inv_n[:, :], inv_n[:, :]), s_dve0))

        pe.wait(raw_in, consts_in)
        act.wait(raw_in, consts_in)
        dve.wait(raw_in, consts_in)
        dve.do(lambda e, _: e.tensor_tensor(l_bias[:, 0:1], l_bias[:, 0:1], l_bias[:, 1:2], ALU.add), s_dve0)
        bank_of = [0]
        banks0 = [Slot(f"setup bank {i}") for i in range(8)]

        def next_bank():
            i = bank_of[0] % 8
            bank_of[0] += 1
            pe.wait_free(banks0[i])
            return i

        def product(rows, lhsTs, rhss, n):
            i = next_bank()
            for k, (a, b) in enumerate(zip(lhsTs, rhss)):
                m = pe.do(lambda e, _, a=a, b=b, k=k: e.matmul(PS[0:rows, i, 0:n], a, b, start=(k == 0), stop=(k == len(lhsTs) - 1)), s_pe0)
            return i, m

        def put_split(hi, lo, src, ready, scale=None):
            act.wait(ready)
            if scale is None:
                h = act.do(lambda e, _: e.activation(hi, src, ACT.Copy), s_act0)
                dve.wait(h)
                return dve.do(lambda e, _: e.tensor_tensor(lo, src, hi.bitcast(F32), ALU.subtract), s_dve0)
            h = act.do(lambda e, _: e.activation(hi, src, ACT.Identity, scale=scale), s_act0)
            dve.wait(h)
            return dve.do(lambda e, _: e.scalar_tensor_tensor(out=lo, in0=src, scalar=scale, in1=hi.bitcast(F32),
                                                              op0=ALU.mult, op1=ALU.subtract), s_dve0)

        turned = []
        for src, dst in ((rWI, tWI), (rWO, tWO), (rR1, tR1)):
            for b in range(DB):
                i = next_bank()
                for a in range(DB):
                    m = pe.do(lambda e, _, a=a, b=b, i=i, src=src: e.transpose(PS[:, i, a * P:(a + 1) * P], src[:, a, b * P:(b + 1) * P], ident[:, :]), s_pe0)
                act.wait(m)
                turned.append(act.do(lambda e, _, b=b, i=i, dst=dst: e.activation(dst[:, b, :], PS[:, i, 0:D], ACT.Copy), s_act0))
                banks0[i].free = [turned[-1]]
        pe.wait(*turned)
        joined = []
        for src, dst in ((rWQ, gQ), (rWK, gK)):
            for f in range(DB):
                i, m = product(P, [tWI[:, e_, f * P:(f + 1) * P] for e_ in range(DB)], [src[:, e_, :] for e_ in range(DB)], D)
                act.wait(m)
                joined.append(act.do(lambda e, _, f=f, i=i, dst=dst: e.activation(dst[:, f, :], PS[:, i, 0:D], ACT.Copy), s_act0))
                banks0[i].free = [joined[-1]]
        i, m = product(P, [ones1], [alpha1], 1)
        dve.wait(m)
        alpha_in = dve.do(lambda e, _, i=i: e.tensor_copy(alphac, PS[:, i, 0:1]), s_dve0)
        banks0[i].free = [alpha_in]
        pe.wait(*joined)
        act.wait(alpha_in)
        dve.wait(alpha_in)
        for left, right, col, n in ((rWQ, rV[0], COL_X, KR), (gQ, rV[1], COL_X + KR, KR), (rWK, rV[2], COL_C, KR),
                                    (gK, rV[3], COL_C + KR, KR), (rWQ, tR1, COL_R, D), (gQ, tR1, COL_R + D, D)):
            for d in range(DB):
                i, m = product(P, [left[:, e_, d * P:(d + 1) * P] for e_ in range(DB)], [right[:, e_, :] for e_ in range(DB)], n)
                banks0[i].free = [put_split(WH[:, d, col:col + n], WL[:, d, col:col + n], PS[:, i, 0:n], m)]
        put_split(WH[:, :, 0:3 * D], WL[:, :, 0:3 * D], rQKV, raw_in)
        put_split(OH[:, :, :], OL[:, :, :], rOUT, raw_in)
        for w in range(2):
            for j in range(KB):
                i, m = product(P, [rU[w][:, e_, j * P:(j + 1) * P] for e_ in range(DB)], [tWO[:, e_, :] for e_ in range(DB)], D)
                banks0[i].free = [put_split(UH[:, KB * w + j, :], UL[:, KB * w + j, :], PS[:, i, 0:D], m,
                                            scale=alphac if w else None)]
        made = []
        for w in range(2):
            i, m = product(KE, [braw[:, w, e_, :] for e_ in range(DB)], [tWO[:, e_, :] for e_ in range(DB)], D)
            dve.wait(m)
            made.append(dve.do(lambda e, _, i=i, w=w: e.tensor_scalar(brow[w], PS[0:KE, i, 0:D], alphac[0:KE, :] if w else 1.0, None, ALU.mult), s_dve0))
            banks0[i].free = [made[-1]]
        i, m = product(1, [bvraw[:, e_:e_ + 1] for e_ in range(DB)], [rOUT[:, e_, :] for e_ in range(DB)], D)
        dve.wait(m)
        made.append(dve.do(lambda e, _, i=i: e.tensor_tensor(brow[2], PS[0:1, i, 0:D], borow, ALU.add), s_dve0))
        banks0[i].free = [made[-1]]
        dve.wait(*made)
        for w in range(3):
            src = brow[w]
            for p in range(3):
                m = dve.do(lambda e, _, w=w, p=p, src=src: e.tensor_copy(bpart[w][p], src), s_dve0)
                dve.wait(m)
                if p < 2:
                    m2 = dve.do(lambda e, _, w=w, p=p, src=src: e.tensor_tensor(brest[w][p], src, bpart[w][p], ALU.subtract), s_dve0)
                    dve.wait(m2)
                    src = brest[w][p]
        sp.wait(m)
        for g in range(6):
            for w in range(2):
                put = sp.do(lambda e, _, g=g, w=w: e.dma_start(bias_rows[HD * g + KE * w:HD * g + KE * (w + 1), :], bpart[w][RIGHT[g]]), s_put0, 16)
        for p in range(3):
            put = sp.do(lambda e, _, p=p: e.dma_start(bias_rows[G16 + p:G16 + p + 1, :], bpart[2][p]), s_put0, 16)
        sp.wait(put)
        setup = (pe, act, dve, pool, sp)
        with nc.Block() as block:
            block.tensor(lambda e: setup[0].write(e))
            block.scalar(lambda e: setup[1].write(e))
            block.vector(lambda e: setup[2].write(e))
            block.gpsimd(lambda e: setup[3].write(e))
            block.sync(lambda e: setup[4].write(e))

        s_ready = tally("stacks_ready")
        with nc.Block() as block:
            @block.vector
            def _(e):
                e.memset(KL[G16:KSTK, :, :], 1.0)
                e.memset(KG[G16:KSTK, :, :], 1.0)
                e.memset(Va[:, :, :, :], 1.0)
                e.memset(craw[:, :, :], 0.0)

        pe, act, dve, pool, sp = (Queue() for _ in range(5))
        names = ("x_in0 x_in1 stat xn turned xhi xlo summed chi clo proj_kq part1 part_dve parts_out kq_in "
                 "projv v_in vs_in vs_zero keys_kept proj_r hidden logits logit_b gate_t gate_max gate_exp gates wt_t wt_in "
                 "xv_ps w_ps cum_ps xv_in xvw xvwc phi plo u_done scores peaks peak_parts peak_turned peak_copied "
                 "peak_out peak_in st exped masked av craw_in ctx_t ctx_rec ctx_tok ctx_f ctx_hi ctx_lo out_ps y stored0 stored1 var0")
        s = {n: tally(n) for n in names.split()}
        bank = [Slot(f"bank {i}") for i in range(8)]
        out_bank = bank[0:2]
        slot = {n: Slot(n) for n in ("tok", "x", "c", "carry", "parts0", "parts1", "parts_d0", "parts_d1", "q", "kl", "kg", "va", "vs",
                                     "logit_f", "gate", "wstack", "wt", "peak", "peak_t", "peak_f", "peak_d", "stats", "junk")}
        rest_slot = [Slot(f"rest {i}") for i in range(2)]
        he_slot = [Slot(f"hidden/exp {i}") for i in range(4)]
        prod_slot = [Slot(f"product {i}") for i in range(3)]
        phl_slot = [Slot(f"split product {i}") for i in range(2)]
        craw_slot = [Slot(f"raw context {i}") for i in range(2)]
        xt_slot = [Slot(f"x {i}") for i in range(2)]

        def psum(i, rows=P, lo=0, hi=512):
            return PS[0:rows, i, lo:hi]

        def three(ps, pairs, first=True, last=True):
            n = len(pairs)
            return [lambda e, _, a=a, b=b, k=k: e.matmul(ps, a, b, start=(first and k == 0), stop=(last and k == n - 1),
                                                         skip_group_check=True) for k, (a, b) in enumerate(pairs)]

        def run_mm(mms, tl):
            for f in mms[:-1]:
                pe.do(f)
            return pe.do(mms[-1], tl)

        def project(i, col, src_h, src_l, tl):
            pairs = []
            for k in range(DB):
                wh, wl = WH[:, k, col:col + P], WL[:, k, col:col + P]
                pairs += [(wh, src_h[:, k, :]), (wh, src_l[:, k, :]), (wl, src_h[:, k, :])]
            pe.wait_free(bank[i])
            return run_mm(three(psum(i), pairs), tl)

        xr = x.rearrange("n (c t p) d -> n c p t d", c=NC, t=T)
        outr = out.rearrange("n (c t p) d -> n c p t d", c=NC, t=T)

        state = {}

        def load_x(c):
            sp.wait_free(xt_slot[c])
            state["x_in", c] = sp.do(lambda e, n: e.dma_start(xt[c], xr[n, c]), s[f"x_in{c}"], 16, apart=True)

        def front(c):
            X = xt[c]
            dve.wait(state["x_in", c])
            dve.wait_free(slot["stats"])
            for t in range(T):
                m = dve.do(lambda e, _, t=t: e.bn_stats(stats[:, t, :], X[:, t, :]), s["stat"])
            dve.wait(m)
            for t in range(T):
                m = dve.do(lambda e, _, t=t: e.bn_aggr(mv[:, t, :], stats[:, t, :]), s["stat"], apart=(t == 0))
            dve.wait(m)
            v, y0, a1, a2, y = (var[:, k, :] for k in (0, 1, 2, 3, 4))
            dve.wait(dve.do(lambda e, _: e.tensor_scalar(v, mv[:, :, 1], LN_EPS, None, ALU.add), s["stat"]))
            m = dve.do(lambda e, _: e.reciprocal(a1, v), s["stat"])
            act.wait(m)
            m = act.do(lambda e, _: e.activation(y0, a1, ACT.Sqrt), s["var0"])
            dve.wait(m)
            dve.wait(dve.do(lambda e, _: e.tensor_tensor(a2, y0, y0, ALU.mult), s["stat"]))
            dve.wait(dve.do(lambda e, _: e.tensor_tensor(a1, a2, v, ALU.mult), s["stat"]))
            dve.wait(dve.do(lambda e, _: e.tensor_scalar(a2, a1, -0.5, 1.5, ALU.mult, ALU.add), s["stat"]))
            dve.wait(dve.do(lambda e, _: e.tensor_tensor(y, a2, y0, ALU.mult), s["stat"]))
            dve.wait_free(slot["tok"])
            for t in range(T):
                m = dve.do(lambda e, _, t=t: e.tensor_scalar(tok[:, t, :], X[:, t, :], mv[:, t, 0:1], var[:, 4, t:t + 1],
                                                             ALU.subtract, ALU.mult), s["xn"])
            slot["stats"].free = [m]
            pe.wait(m)
            for k in range(DB):
                i = 2 + k
                pe.wait_free(bank[i])
                for t in range(T):
                    mt = pe.do(lambda e, _, t=t, k=k, i=i: e.transpose(psum(i, lo=t * P, hi=(t + 1) * P), tok[:, t, k * P:(k + 1) * P], ident[:, :]), s["turned"])
                act.wait(mt)
                if k == 0:
                    act.wait_free(slot["x"])
                mh = act.do(lambda e, _, k=k, i=i: e.activation(XH[:, k, :], psum(i), ACT.Copy), s["xhi"])
                dve.wait(mh)
                ml = dve.do(lambda e, _, k=k, i=i: e.tensor_tensor(XL[:, k, :], psum(i), XH[:, k, :].bitcast(F32), ALU.subtract), s["xlo"])
                dve.wait_free(rest_slot[k])
                if c:
                    dve.wait_free(slot["carry"])
                init = carry[:, k:k + 1] if c else 0.0
                ms = dve.do(lambda e, _, k=k, i=i, init=init: e.tensor_tensor_scan(rest[:, k, :], psum(i), psum(i), init, ALU.add, ALU.bypass)
                            if False else e.tensor_tensor_scan(rest[:, k, :], psum(i), XH[:, k, :].bitcast(F32), init, ALU.add, ALU.bypass), s["summed"])
                bank[i].free = [ms]
                act.wait(ms)
                if k == 0:
                    act.wait_free(slot["c"])
                    pool.wait_free(slot["c"])
                mch = act.do(lambda e, _, k=k: e.activation(CH[:, k, :], rest[:, k, :], ACT.Copy), s["chi"])
                pool.wait(mch)
                mcl = pool.do(lambda e, _, k=k: e.tensor_tensor(CL[:, k, :], rest[:, k, :], CH[:, k, :].bitcast(F32), ALU.subtract), s["clo"])
                if c == 0:
                    dve.wait(ms)
                    mc = dve.do(lambda e, _, k=k: e.tensor_copy(carry[:, k:k + 1], rest[:, k, C - 1:C]), s["summed"])
                    slot["carry"].free = [mc]
                    rest_slot[k].free = [mcl, mc]
                else:
                    rest_slot[k].free = [mcl]
            slot["tok"].free = [mt]
            state["x"] = (mh, ml)
            state["c"] = (mch, mcl)

        def keys_queries(c):
            pe.wait(*state["x"])
            n = 0
            for w, col, bias in ((1, COL_K, k_bias), (0, COL_Q, q_bias)):
                act.wait_free(slot[f"parts{w}"])
                dve.wait_free(slot[f"parts{w}"])
                for b in range(DB):
                    i = 4 + n % 4
                    r = n % 2
                    n += 1
                    m = project(i, col + b * P, XH, XL, s["proj_kq"])
                    p1, p2, p3 = (parts[:, w, j, b, :] for j in range(3))
                    R_ = rest[:, r, :]
                    act.wait(m)
                    m1 = act.do(lambda e, _, i=i, b=b, bias=bias, p1=p1: e.activation(p1, psum(i), ACT.Identity, bias=bias[:, b:b + 1]), s["part1"])
                    dve.wait(m1)
                    dve.wait_free(rest_slot[r])
                    m2 = dve.do(lambda e, _, i=i, b=b, bias=bias, p1=p1, R_=R_: e.scalar_tensor_tensor(
                        out=R_, in0=psum(i), scalar=bias[:, b:b + 1], in1=p1, op0=ALU.add, op1=ALU.subtract), s["part_dve"])
                    bank[i].free = [m2]
                    dve.wait(m2)
                    m3 = dve.do(lambda e, _, p2=p2, R_=R_: e.tensor_copy(p2, R_), s["part_dve"])
                    dve.wait(m3)
                    m4 = dve.do(lambda e, _, p2=p2, p3=p3, R_=R_: e.tensor_tensor(p3, R_, p2, ALU.subtract), s["part_dve"])
                    rest_slot[r].free = [m4]
                state["parts", w] = (m1, m4)
            dve.wait_free(slot["kl"])
            if c == 0:
                mk = dve.do(lambda e, _: e.memset(KL[0:KSTK, :, 0:WINDOW], 0.0), s["keys_kept"])
            else:
                mk = dve.do(lambda e, _: e.tensor_copy(KL[0:KSTK, :, 0:WINDOW], KL[0:KSTK, :, C:C + WINDOW]), s["keys_kept"])
            state["kept"] = mk
            for w in (1, 0):
                sp.wait(*state["parts", w])
                sp.wait_free(slot[f"parts_d{w}"])
                mo = sp.do(lambda e, _, w=w: e.dma_start(parts_d[w].rearrange("i (b p) t -> p i b t", p=P), parts[:, w, :, :, :]), s["parts_out"], 16)
                slot[f"parts{w}"].free = [mo]
                sp.wait(mo)
                if w:
                    sp.wait(mk)
                    sp.wait_free(slot["kl"])
                    sp.wait_free(slot["kg"])
                else:
                    sp.wait_free(slot["q"])
                for g in range(6):
                    rows = slice(HD * g, HD * (g + 1))
                    src = parts_d[w, (LEFT if w else RIGHT)[g]].rearrange("(h d) t -> d h t", d=HD)
                    if w:
                        sp.do(lambda e, _, rows=rows, src=src: e.dma_start(KL[rows, :, WINDOW:], src[:, NG:, :]), s["kq_in"], 16)
                        mi = sp.do(lambda e, _, rows=rows, src=src: e.dma_start(KG[rows, :, c * C:(c + 1) * C], src[:, 0:NG, :]), s["kq_in"], 16)
                    else:
                        mi = sp.do(lambda e, _, rows=rows, src=src: e.dma_start(QS[rows, :, :], src), s["kq_in"], 16)
                slot[f"parts_d{w}"].free = [mi]
            state["kq"] = mi

        def values(c):
            act.wait_free(slot["va"])
            for u in range(T // 2):
                i = 2 + u
                pe.wait_free(bank[i])
                for a in range(2):
                    t = 2 * u + a
                    pairs = []
                    for k in range(DB):
                        wh, wl = WH[:, k, COL_V:COL_V + D], WL[:, k, COL_V:COL_V + D]
                        xh, xl = XH[:, k, t * P:(t + 1) * P], XL[:, k, t * P:(t + 1) * P]
                        pairs += [(xh, wh), (xh, wl), (xl, wh)]
                    m = run_mm(three(psum(i, lo=a * D, hi=(a + 1) * D), pairs), s["projv"])
                act.wait(m)
                tt = c * T + 2 * u
                mv_ = act.do(lambda e, _, i=i, tt=tt: e.activation(
                    Va[:, tt:tt + 2, :, 0:HD], psum(i).rearrange("p (a h d) -> p a h d", a=2, h=NH), ACT.Copy), s["v_in"])
                bank[i].free = [mv_]
            state["v"] = mv_
            sp.wait(mv_)
            sp.wait_free(slot["vs"])
            t0 = c * T
            if c == 0:
                pool.wait_free(slot["vs"])
                mz = pool.do(lambda e, _: e.memset(Vs[0:WINDOW, 0, :, :], 0.0), s["vs_zero"], apart=True)
                state["vs_zero"] = mz
                sp.do(lambda e, _: e.dma_start(Vs[0:WINDOW, 1:T, :, :], Va[WINDOW:P, 0:T - 1, NG:, :]), s["vs_in"], 16)
            else:
                sp.do(lambda e, _: e.dma_start(Vs[0:WINDOW, :, :, :], Va[WINDOW:P, t0 - 1:t0 + T - 1, NG:, :]), s["vs_in"], 16)
            state["vs"] = sp.do(lambda e, _: e.dma_start(Vs[WINDOW:P, :, :, :], Va[0:WINDOW, t0:t0 + T, NG:, :]), s["vs_in"], 16)

        def router(c):
            for j in range(2 * DB):
                i = 4 + j
                m = project(i, COL_R + j * P, XH, XL, s["proj_r"])
                act.wait(m)
                act.wait_free(he_slot[j])
                mh = act.do(lambda e, _, i=i, j=j: e.activation(HE[:, j, :], psum(i), ACT.Gelu, bias=r_bias[:, j % DB:j % DB + 1]), s["hidden"])
                bank[i].free = [mh]
            pe.wait(mh)
            pe.wait_free(bank[2])
            for j in range(2 * DB):
                m = pe.do(lambda e, _, j=j: e.matmul(psum(2, rows=2 * KE), W2[:, j, :], HE[:, j, :], start=(j == 0), stop=(j == 2 * DB - 1)), s["logits"])
                he_slot[j].free = [m]
            act.wait(m)
            act.wait_free(slot["logit_f"])
            ml = act.do(lambda e, _: e.activation(logit_f[:, :], psum(2, rows=2 * KE), ACT.Identity, bias=l_bias[:, 0:1]), s["logit_b"])
            bank[2].free = [ml]
            pe.wait(ml)
            pe.wait_free(bank[3])
            for t in range(T):
                m = pe.do(lambda e, _, t=t: e.transpose(psum(3, lo=t * 2 * KE, hi=(t + 1) * 2 * KE), logit_f[:, t * P:(t + 1) * P],
                                                        ident[0:2 * KE, 0:2 * KE]), s["gate_t"], apart=(t == 0))
            slot["logit_f"].free = [m]
            lg = psum(3, hi=T * 2 * KE).rearrange("p (a k) -> p a k", k=KE)
            g4 = [gate[:, k, :, :].rearrange("p t (w k) -> p (t w) k", k=KE) for k in range(4)]
            dve.wait(m)
            dve.wait_free(slot["gate"])
            dve.wait(dve.do(lambda e, _: e.tensor_reduce(gsum[:, 0, :], lg, AX_X, ALU.max), s["gate_max"]))
            m = dve.do(lambda e, _: e.tensor_tensor(g4[0], lg, gsum[:, 0, :].unsqueeze(2).to_broadcast([P, 2 * T, KE]), ALU.subtract), s["gate_max"])
            bank[3].free = [m]
            act.wait(m)
            m = act.do(lambda e, _: e.activation(g4[1], g4[0], ACT.Exp), s["gate_exp"])
            dve.wait(m)
            dve.wait(dve.do(lambda e, _: e.tensor_reduce(gsum[:, 1, :], g4[1], AX_X, ALU.add), s["gates"]))
            dve.wait(dve.do(lambda e, _: e.reciprocal(gsum[:, 2, :], gsum[:, 1, :]), s["gates"]))
            dve.wait(dve.do(lambda e, _: e.tensor_tensor(
                gsum[:, 3, :].rearrange("p (t w) -> p t w", w=2), gsum[:, 2, :].rearrange("p (t w) -> p t w", w=2),
                inv_n[:, c * T:(c + 1) * T].unsqueeze(2).to_broadcast([P, T, 2]), ALU.mult), s["gates"]))
            dve.wait(dve.do(lambda e, _: e.tensor_tensor(g4[2], g4[1], gsum[:, 3, :].unsqueeze(2).to_broadcast([P, 2 * T, KE]), ALU.mult), s["gates"]))
            dve.wait_free(slot["wstack"])
            ws = wstack[:, :, 0:G16].rearrange("p t (g k) -> p t g k", k=2 * KE)
            w_f, w_r = gate[:, 2], gate[:, 3]

            def copies(src, n):
                return src.unsqueeze(2).to_broadcast([P, T, n, 2 * KE])

            dve.wait(dve.do(lambda e, _: e.tensor_copy(ws[:, :, 0:3, :], copies(w_f, 3)), s["gates"]))
            dve.wait(dve.do(lambda e, _: e.tensor_tensor(w_r, w_f, ws[:, :, 0, :], ALU.subtract), s["gates"]))
            dve.wait(dve.do(lambda e, _: e.tensor_copy(ws[:, :, 3:5, :], copies(w_r, 2)), s["gates"]))
            m = dve.do(lambda e, _: e.tensor_tensor(ws[:, :, 5, :], w_r, ws[:, :, 3, :], ALU.subtract), s["gates"])
            slot["gate"].free = [m]
            pe.wait(m)
            pe.wait_free(bank[4])
            wt_ps = PS[0:KSTK, 4, :].bitcast(BF16)
            for t in range(T):
                m = pe.do(lambda e, _, t=t: e.transpose(wt_ps[:, t * P:(t + 1) * P], wstack[:, t, :], ident_b[:, :]), s["wt_t"])
            slot["wstack"].free = [m]
            act.wait(m)
            act.wait_free(slot["wt"])
            m = act.do(lambda e, _: e.activation(WT[:, :], wt_ps[:, 0:C], ACT.Copy), s["wt_in"])
            bank[4].free = [m]
            state["wt"] = m

        def out_ps(t):
            return psum(t // 2, lo=(t % 2) * D, hi=(t % 2 + 1) * D)

        def open_out(c):
            pe.wait(state["wt"])
            for t in range(T):
                if t % 2 == 0:
                    pe.wait_free(bank[t // 2])
                pe.do(lambda e, _, t=t: e.matmul(out_ps(t), WT[:, t * P:(t + 1) * P], bias_rows[:, :], start=(t % 2 == 0), stop=False,
                                                 skip_group_check=True))

        def expert(c, j):
            r, h = j % 3, j % 2
            if j == 0:
                pe.wait(*state["c"])
            m_x = project(2, COL_X + j * P, XH, XL, s["xv_ps"])
            pe.wait_free(bank[4])
            m_w = pe.do(lambda e, _: e.matmul(psum(4), spread[:, j, :], WT[:, :], start=True, stop=True), s["w_ps"])
            m_c = project(3, COL_C + j * P, CH, CL, s["cum_ps"])
            act.wait(m_x)
            act.wait_free(prod_slot[r])
            m = act.do(lambda e, _: e.activation(prod[:, r, :], psum(2), ACT.Copy), s["xv_in"])
            bank[2].free = [m]
            dve.wait(m, m_w)
            m = dve.do(lambda e, _: e.tensor_tensor(prod[:, r, :], psum(4), prod[:, r, :], ALU.mult), s["xvw"])
            bank[4].free = [m]
            dve.wait(m, m_c)
            m = dve.do(lambda e, _: e.tensor_tensor(prod[:, r, :], psum(3), prod[:, r, :], ALU.mult), s["xvwc"])
            bank[3].free = [m]
            act.wait(m)
            act.wait_free(phl_slot[h])
            mh = act.do(lambda e, _: e.activation(PH[:, h, :], prod[:, r, :], ACT.Copy), s["phi"])
            pool.wait(mh)
            pool.wait_free(phl_slot[h])
            ml = pool.do(lambda e, _: e.tensor_tensor(PL[:, h, :], prod[:, r, :], PH[:, h, :].bitcast(F32), ALU.subtract), s["plo"])
            prod_slot[r].free = [ml]
            state["p", j] = (mh, ml)
            if j == 2 * KB - 1:
                slot["wt"].free = [m_w]
                slot["x"].free = [m_x]
                slot["c"].free = [m_c]

        def mix(c, j):
            h = j % 2
            mh, ml = state["p", j]
            pe.wait(mh)
            for part, uu in ((PH, (UH, UL)), (PL, (UH,))):
                if part is PL:
                    pe.wait(ml)
                for t in range(T):
                    for u in uu:
                        m = pe.do(lambda e, _, t=t, part=part, u=u: e.matmul(
                            out_ps(t), part[:, h, t * P:(t + 1) * P], u[:, j, :], start=False, stop=False, skip_group_check=True), s["u_done"])
            phl_slot[h].free = [m]

        def peaks_local(c, t, pair):
            i = state["sbank"] = 11 - state.get("sbank", 6)
            pe.wait(state["kq"], state["kept"])
            pe.wait_free(bank[i])
            for a in range(2):
                l = 2 * pair + a
                m = pe.do(lambda e, _, a=a, l=l: e.matmul(psum(i, lo=256 * a, hi=256 * a + BW), QS[0:G16, NG + l, t * P:(t + 1) * P],
                                                          KL[0:G16, l, t * P:t * P + BW], start=(a == 0), stop=(a == 1),
                                                          skip_group_check=True), s["scores"])
            dve.wait(m)
            if t == 0 and pair == 0:
                dve.wait_free(slot["peak"])
            which = 1 if c == 0 and t == 0 else 0
            for a in range(2):
                h = NG + 2 * pair + a
                m = dve.do(lambda e, _, a=a, h=h: e.tensor_tensor_reduce(
                    psum(i, lo=256 * a, hi=256 * a + BW), psum(i, lo=256 * a, hi=256 * a + BW), band[:, which, :], 1.0, LOWEST, ALU.add, ALU.max,
                    peak[:, t, h:h + 1]), s["peaks"], apart=(a == 0))
            bank[i].free = [m]
            state["peaks"] = m

        def peaks_global(c, t, g):
            start = LOWEST
            for q in range(c + 1):
                i = state["sbank"] = 11 - state.get("sbank", 6)
                n = C if q < c else (t + 1) * P
                pe.wait(state["kq"])
                pe.wait_free(bank[i])
                m = pe.do(lambda e, _, q=q, n=n, i=i: e.matmul(psum(i, hi=n), QS[0:G16, g, t * P:(t + 1) * P], KG[0:G16, g, q * C:q * C + n],
                                                               start=True, stop=True), s["scores"])
                dve.wait(m)
                if q < c:
                    m = dve.do(lambda e, _, i=i: e.tensor_reduce(peak_part[:, t, g:g + 1], psum(i), AX_X, ALU.max), s["peak_parts"])
                    bank[i].free = [m]
                    dve.wait(m)
                    start = peak_part[:, t, g:g + 1]
                else:
                    m = dve.do(lambda e, _, n=n, i=i, start=start: e.tensor_tensor_reduce(
                        psum(i, hi=n), psum(i, hi=n), strip[:, C - n:C], 1.0, start, ALU.add, ALU.max, peak[:, t, g:g + 1]), s["peaks"], apart=True)
                    bank[i].free = [m]
            state["peaks"] = m

        def peaks_to_rows(c):
            pt = [peak_t[:, :, k * NH:(k + 1) * NH] for k in range(3)]
            dve.wait(state["peaks"])
            dve.wait_free(slot["peak_t"])
            dve.wait(dve.do(lambda e, _: e.tensor_scalar(pt[0], peak[:, :, :], -1.0, None, ALU.mult), s["peak_parts"]))
            dve.wait(dve.do(lambda e, _: e.scalar_tensor_tensor(out=peak_rest[:, 0], in0=peak[:, :, :], scalar=-1.0, in1=pt[0],
                                                                op0=ALU.mult, op1=ALU.subtract), s["peak_parts"]))
            dve.wait(dve.do(lambda e, _: e.tensor_copy(pt[1], peak_rest[:, 0]), s["peak_parts"]))
            m = dve.do(lambda e, _: e.tensor_tensor(pt[2], peak_rest[:, 0], pt[1], ALU.subtract), s["peak_parts"])
            slot["peak"].free = [m]
            pe.wait(m)
            pe.wait_free(bank[7])
            ps = PS[0:3 * NH, 7, :].bitcast(BF16)
            for t in range(T):
                m = pe.do(lambda e, _, t=t: e.transpose(ps[:, t * P:(t + 1) * P], peak_t[:, t, :], ident_b[:, :]), s["peak_turned"], apart=(t == 0))
            slot["peak_t"].free = [m]
            act.wait(m)
            act.wait_free(slot["peak_f"])
            m = act.do(lambda e, _: e.activation(peak_f[:, :], ps[:, 0:C], ACT.Copy), s["peak_copied"])
            bank[7].free = [m]
            sp.wait(m)
            sp.wait_free(slot["peak_d"])
            m = sp.do(lambda e, _: e.dma_start(peak_d, peak_f[:, :]), s["peak_out"], 16)
            slot["peak_f"].free = [m]
            sp.wait(m)
            m = sp.do(lambda e, _: e.dma_start(QS[G16:KSTK, :, :], peak_d.rearrange("(a h) t -> a h t", h=NH)), s["peak_in"], 16)
            slot["peak_d"].free = [m]
            state["peak_in"] = m

        def next_exp():
            k = state["exp"] = (state.get("exp", -1) + 1) % 4
            return k

        def attend_local(c, l):
            h, grp, g = NG + l, 1 + l // 4, l % 4
            cb = 7 if grp % 2 else 4
            i = state["sbank"] = 11 - state.get("sbank", 6)
            pe.wait(state["peak_in"])
            pe.wait_free(bank[i])
            for w in range(8):
                m = pe.do(lambda e, _, w=w: e.matmul(psum(i, lo=w * WINDOW, hi=(w + 1) * WINDOW), KL[0:KSTK, l, w * WINDOW:w * WINDOW + P],
                                                     QS[0:KSTK, h, w * WINDOW:(w + 1) * WINDOW], start=(w == 0), stop=(w == 7),
                                                     skip_group_check=True), s["st"])
            k = next_exp()
            act.wait(m)
            act.wait_free(he_slot[k])
            m = act.do(lambda e, _: e.activation(HE[:, k, :], psum(i), ACT.Exp, scale=SCALE), s["exped"])
            bank[i].free = [m]
            ev = HE[:, k, :].rearrange("p (w q) -> p w q", w=8)
            for pattern, base, cm in (([[0, 8], [-1, WINDOW]], 0, 1), ([[0, 8], [1, WINDOW]], WINDOW, -1)):
                pool.wait(m)
                m = pool.do(lambda e, _, pattern=pattern, base=base, cm=cm: e.affine_select(
                    out=ev, in_=ev, compare_op=ALU.is_ge, fill=0.0, base=base, pattern=pattern, channel_multiplier=cm), s["masked"], apart=True)

            def av():
                pe.wait(m, state["v"], state["vs"])
                if c == 0:
                    pe.wait(state["vs_zero"])
                if g == 0:
                    pe.wait_free(bank[cb])
                for w in range(8):
                    v = Vs[:, w // 2, l, :] if w % 2 == 0 else Va[:, c * T + w // 2, h, :]
                    q = slice(w * WINDOW, (w + 1) * WINDOW)
                    m2 = pe.do(lambda e, _, v=v, q=q, w=w: e.matmul(PS[32 * g:32 * g + VW, cb, q], v, HE[:, k, q], start=(w == 0), stop=(w == 7),
                                                               skip_group_check=True), s["av"])
                he_slot[k].free = [m2]
                if g == 3:
                    state["ctx", grp] = (m2, cb)
            return av

        def attend_global(c, g, j):
            lo = max(0, (j - c * T) * P)
            i = state["sbank"] = 11 - state.get("sbank", 6)
            pe.wait(state["peak_in"])
            pe.wait_free(bank[i])
            m = pe.do(lambda e, _: e.matmul(psum(i, lo=lo), KG[0:KSTK, g, j * P:(j + 1) * P], QS[0:KSTK, g, lo:C], start=True, stop=True), s["st"])
            k = next_exp()
            act.wait(m)
            act.wait_free(he_slot[k])
            m = act.do(lambda e, _: e.activation(HE[:, k, lo:C], psum(i, lo=lo), ACT.Exp, scale=SCALE), s["exped"])
            bank[i].free = [m]
            if j >= c * T:
                pool.wait(m)
                ev = HE[:, k, lo:lo + P]
                m = pool.do(lambda e, _: e.affine_select(out=ev, in_=ev, compare_op=ALU.is_ge, fill=0.0, base=0, pattern=[[1, P]],
                                                         channel_multiplier=-1), s["masked"], apart=True)
            last = j == (c + 1) * T - 1

            def av():
                pe.wait(m, state["v"])
                if g == 0 and j == 0:
                    pe.wait_free(bank[4])
                m2 = pe.do(lambda e, _: e.matmul(PS[32 * g:32 * g + VW, 4, lo:C], Va[:, j, g, :], HE[:, k, lo:C], start=(j == 0), stop=last,
                                                 skip_group_check=True), s["av"])
                he_slot[k].free = [m2]
                if g == 3 and last:
                    state["ctx", 0] = (m2, 4)
            return av

        def context(c, grp):
            m, cb = state["ctx", grp]
            r = grp % 2
            act.wait(m)
            act.wait_free(craw_slot[r])
            m = act.do(lambda e, _: e.activation(craw[:, r, :], psum(cb), ACT.Copy), s["craw_in"])
            bank[cb].free = [m]
            tb = 2 + r
            pe.wait(m)
            pe.wait_free(bank[tb])
            for t in range(T):
                m = pe.do(lambda e, _, t=t: e.transpose(psum(tb, lo=t * P, hi=(t + 1) * P), craw[:, r, t * P:(t + 1) * P], ident[:, :]), s["ctx_t"])
            craw_slot[r].free = [m]
            raw_t = psum(tb).rearrange("p (t g e) -> p t g e", t=T, g=4)
            dve.wait(m)
            if grp == 1:
                dve.wait_free(slot["tok"])
            dve.wait(dve.do(lambda e, _: e.reciprocal(cinv[:, r, :, :], raw_t[:, :, :, HD]), s["ctx_rec"]))
            m = dve.do(lambda e, _: e.tensor_tensor(
                tok[:, :, grp * 64:(grp + 1) * 64].rearrange("p t (g d) -> p t g d", g=4), raw_t[:, :, :, 0:HD],
                cinv[:, r, :, :].unsqueeze(3).to_broadcast([P, T, 4, HD]), ALU.mult), s["ctx_tok"])
            bank[tb].free = [m]
            state["tok"] = m

        def finish(c):
            pe.wait(state["tok"])
            act.wait_free(slot["c"])
            for k in range(DB):
                i = 2 + k
                pe.wait_free(bank[i])
                for t in range(T):
                    m = pe.do(lambda e, _, t=t, k=k, i=i: e.transpose(psum(i, lo=t * P, hi=(t + 1) * P), tok[:, t, k * P:(k + 1) * P], ident[:, :]), s["ctx_f"])
                act.wait(m)
                mh = act.do(lambda e, _, k=k, i=i: e.activation(CH[:, k, :], psum(i), ACT.Copy), s["ctx_hi"])
                dve.wait(mh)
                ml = dve.do(lambda e, _, k=k, i=i: e.tensor_tensor(CL[:, k, :], psum(i), CH[:, k, :].bitcast(F32), ALU.subtract), s["ctx_lo"])
                bank[i].free = [ml]
            slot["tok"].free = [m]
            pe.wait(mh, ml)
            X = xt[c]
            for u in range(T // 2):
                for t in (2 * u, 2 * u + 1):
                    for k in range(DB):
                        for a, b in ((CH, OH), (CH, OL), (CL, OH)):
                            m = pe.do(lambda e, _, t=t, k=k, a=a, b=b: e.matmul(
                                out_ps(t), a[:, k, t * P:(t + 1) * P], b[:, k, :], start=False,
                                stop=(k == DB - 1 and a is CL), skip_group_check=True), s["out_ps"])
                dve.wait(m)
                my = dve.do(lambda e, _, u=u: e.tensor_tensor(X[:, 2 * u:2 * u + 2, :], psum(u).rearrange("p (a d) -> p a d", a=2),
                                                              X[:, 2 * u:2 * u + 2, :], ALU.add), s["y"])
                bank[u].free = [my]
            slot["c"].free = [m]
            sp.wait(my)
            mo = sp.do(lambda e, n: e.dma_start(outr[n, c], X), s[f"stored{c}"], 16, apart=True)
            xt_slot[c].free = [mo]

        load_x(0)
        load_x(1)
        for c in range(NC):
            front(c)
            keys_queries(c)
            router(c)
            values(c)
            open_out(c)
            units = [(peaks_local, t, p) for t in range(T) for p in range(NL // 2)] + [(peaks_global, t, g) for t in range(T) for g in range(NG)]
            expert(c, 0)
            expert(c, 1)
            mix(c, 0)
            done = 0
            for j in range(2, 6):
                expert(c, j)
                upto = len(units) * (j - 1) // 4
                for f, t, a in units[done:upto]:
                    f(c, t, a)
                done = upto
                mix(c, j - 1)
            peaks_to_rows(c)
            for j in range(6, 8):
                expert(c, j)
                mix(c, j - 1)
            late = []

            def step(av):
                late.append(av)
                if len(late) > 2:
                    late.pop(0)()

            for grp in range(1, 1 + NL // 4):
                for l in range(4 * grp - 4, 4 * grp):
                    step(attend_local(c, l))
                if grp == 1:
                    mix(c, 7)
                while late:
                    late.pop(0)()
                context(c, grp)
            for g in range(NG):
                for j in range((c + 1) * T):
                    step(attend_global(c, g, j))
            while late:
                late.pop(0)()
            context(c, 0)
            slot["q"].free = [Mark(s["st"], s["st"].n)]
            slot["kl"].free = slot["q"].free
            slot["kg"].free = slot["q"].free
            slot["va"].free = [Mark(s["av"], s["av"].n), state["vs"]]
            slot["vs"].free = [Mark(s["av"], s["av"].n)]
            finish(c)

        with nc.Block() as block:
            @block.sync
            def _(e):
                for t_ in s.values():
                    if t_.n:
                        e.sem_inc(t_.sem, t_.n)

        body = (pe, act, dve, pool, sp)

        def looped(queue):
            def program(e):
                with e.Fori(0, NB) as n:
                    queue.write(e, n, waits_apart=queue is sp)
                if queue is sp:
                    for c in range(NC):
                        e.wait_ge(s[f"stored{c}"].sem, s[f"stored{c}"].n * (NB + 1))
            return program

        with nc.Block() as block:
            block.tensor(looped(body[0]))
            block.scalar(looped(body[1]))
            block.vector(looped(body[2]))
            block.gpsimd(looped(body[3]))
            block.sync(looped(body[4]))


_INS = ['L0_attn_x', 'L0_attn_w_qkv', 'L0_attn_b_qkv', 'L0_attn_w_out', 'L0_attn_b_out', 'L0_ffn_W_Q', 'L0_ffn_W_K',
        'L0_ffn_W_O', 'L0_ffn_W_inv', 'L0_ffn_V_fwd', 'L0_ffn_W_fwd', 'L0_ffn_U_fwd', 'L0_ffn_b_fwd', 'L0_ffn_V_inv',
        'L0_ffn_W_inv_exp', 'L0_ffn_U_inv', 'L0_ffn_b_inv', 'L0_ffn_router_w1', 'L0_ffn_router_b1', 'L0_ffn_router_w2',
        'L0_ffn_router_b2', 'L0_ffn_alpha_bi', 'L0_ffn_expert_bias']


def kernel(**inputs):
    import numpy as _np
    import concourse.bacc as _bacc
    from concourse import mybir as _mybir
    from concourse.bass_utils import run_bass_kernel_spmd as _run

    nc = _bacc.Bacc("TRN2", target_bir_lowering=False, num_devices=1)
    arrays, args = {}, []
    for name in _INS:
        a = _np.ascontiguousarray(inputs[name])
        if a.ndim == 0:
            a = a.reshape(1)
        arrays[f"in_{name}_dram"] = a
        args.append(nc.dram_tensor(f"in_{name}_dram", a.shape, _mybir.dt.from_np(a.dtype), kind="ExternalInput").ap())
    shape = tuple(inputs['L0_attn_x'].shape)
    args.append(nc.dram_tensor("out_0_dram", shape, _mybir.dt.float32, kind="ExternalOutput").ap())
    with nc.allow_non_contiguous_dma("small weights are read by columns once"):
        mixer_layer(nc, *args)
    r = _run(nc, [arrays], core_ids=[0])
    return r.results[0]["out_0_dram"]
```

```python
from contextlib import ExitStack

import concourse.bass as bass
from concourse import mybir

F32 = mybir.dt.float32
F32R = mybir.dt.float32r
BF16 = mybir.dt.bfloat16
I32 = mybir.dt.int32
ALU = mybir.AluOpType
ACT = mybir.ActivationFunctionType
AX_X = mybir.AxisListType.X

P = 128
WINDOW = 64
N_GLOBAL = 4
LN_EPS = 1e-5
MASKED = -1e30
LOWEST = -3e38


class Tally:

    def __init__(self, sem):
        self.sem = sem
        self.n = 0


class Mark:

    def __init__(self, tally, value):
        self.tally, self.value = tally, value


class Latest:

    def __init__(self, name):
        self.name, self.marks = name, []


class Queue:

    def __init__(self):
        self.items = []

    def wait(self, *marks):
        for m in marks:
            self.items.append(("wait", m))

    def wait_latest(self, thing):
        if thing.marks:
            self.wait(*thing.marks)
        else:
            self.items.append(("wait_last_turn", thing))

    def do(self, fn, tally=None, by=1, apart=False):
        if apart:
            self.items.append(("do", lambda e, _: e.nop(nofuse=True), None, 0))
        if tally is None:
            self.items.append(("do", fn, None, 0))
            return None
        tally.n += by
        self.items.append(("do", fn, tally, by))
        return Mark(tally, tally.n)

    def write(self, eng, turn=None, waits_apart=False):
        seen, due = {}, {}
        for item in self.items:
            if item[0] == "wait":
                due[item[1].tally] = max(item[1].value, due.get(item[1].tally, -(1 << 30)))
            elif item[0] == "wait_last_turn":
                for m in item[1].marks if turn is not None else ():
                    due[m.tally] = max(m.value - m.tally.n, due.get(m.tally, -(1 << 30)))
            else:
                for tally, value in due.items():
                    if seen.get(tally, -(1 << 30)) < value:
                        seen[tally] = value
                        eng.wait_ge(tally.sem, value if turn is None else turn * tally.n + (tally.n + value))
                        if waits_apart:
                            eng.nop(nofuse=True)
                due = {}
                _, fn, tally, by = item
                ins = fn(eng, turn)
                if tally is not None:
                    ins.then_inc(tally.sem, by)
        for tally, value in due.items():
            eng.wait_ge(tally.sem, value if turn is None else turn * tally.n + (tally.n + value))


def mixer_layer(
    nc, x, w_qkv, b_qkv, w_out, b_out, W_Q, W_K, W_O, W_inv, V_fwd, W_fwd, U_fwd, b_fwd,
    V_inv, W_inv_exp, U_inv, b_inv, router_w1, router_b1, router_w2, router_b2, alpha, expert_bias, out,
):
    NB, S, D = x.shape
    KE, _, R = V_fwd.shape
    HD = 16
    NH = D // HD
    NG = N_GLOBAL
    NL = NH - NG
    KR = KE * R
    DB = D // P
    KB = KR // P
    C = 512
    NC = S // C
    T = C // P
    ST = S // P
    SCALE = float(HD) ** -0.5
    assert DB == 2 and NC == 2 and KR == 512 and NG == 4 and NL % 4 == 0 and C // WINDOW == 8
    COL_Q, COL_K, COL_V = 0, D, 2 * D
    COL_R = 3 * D
    COL_X = COL_R + 2 * D
    COL_C = COL_X + 2 * KR
    NCOL = COL_C + 2 * KR
    G16 = 6 * HD
    KSTK = G16 + 3
    LEFT, RIGHT = (0, 0, 0, 1, 1, 2), (0, 1, 2, 0, 1, 0)
    VW = HD + 1

    ctx = ExitStack()
    with ctx:
        def sb(name, shape, dt=F32):
            return ctx.enter_context(nc.sbuf_tensor(name, shape, dt))

        def tally(name):
            return Tally(ctx.enter_context(nc.semaphore(name)))

        WH = sb("WH", [P, DB, NCOL], F32R)
        WL = sb("WL", [P, DB, NCOL], F32R)
        UH = sb("UH", [P, 2 * KB, D], F32R)
        UL = sb("UL", [P, 2 * KB, D], F32R)
        OH = sb("OH", [P, DB, D], F32R)
        OL = sb("OL", [P, DB, D], F32R)
        bias_rows = sb("bias_rows", [KSTK, D], BF16)
        spread = sb("spread", [KSTK, 2 * KB, P], BF16)
        W2 = sb("W2", [P, DB, KE])
        ident = sb("ident", [P, P])
        ident_b = sb("ident_b", [P, P], BF16)
        band = sb("band", [P, 2, P + WINDOW])
        strip = sb("strip", [P, C])
        q_bias = sb("q_bias", [P, DB])
        k_bias = sb("k_bias", [P, DB])
        r_bias = sb("r_bias", [P, DB])
        l_bias = sb("l_bias", [P, 2])
        inv_n = sb("inv_n", [P, ST])

        QS_W = NH * C // 2
        KL_W = NL * (C + WINDOW) // 2
        KG_W = NG * S // 2
        PT_W = 2 * 3 * DB * C // 2
        AREA = QS_W + KL_W + KG_W + PT_W
        area = sb("area", [P, AREA])
        at = [0]

        def carve(width):
            a = area[:, at[0]:at[0] + width]
            at[0] += width
            return a

        QS = carve(QS_W).bitcast(BF16).rearrange("p (h t) -> p h t", h=NH)
        KL = carve(KL_W).bitcast(BF16).rearrange("p (h t) -> p h t", h=NL)
        KG = carve(KG_W).bitcast(BF16).rearrange("p (h t) -> p h t", h=NG)
        parts = carve(PT_W).bitcast(BF16).rearrange("p (w i b t) -> p w i b t", w=2, i=3, b=DB)

        xt = [sb(f"xt{i}", [P, T, D]) for i in range(2)]
        tok = sb("tok", [P, T, D])
        XH = sb("XH", [P, DB, C], F32R)
        XL = sb("XL", [P, DB, C], F32R)
        CH = sb("CH", [P, DB, C], F32R)
        CL = sb("CL", [P, DB, C], F32R)
        rest = sb("rest", [P, 2, C])
        carry = sb("carry", [P, DB])
        stats = sb("stats", [P, T, 6])
        mv = sb("mv", [P, T, 2])
        var = sb("var", [P, 6, T])
        Va = sb("Va", [P, ST, NH, VW])
        Vs = sb("Vs", [P, T, NL, VW])
        HE = sb("HE", [P, 4, C])
        gate = sb("gate", [P, 4, T, 2 * KE])
        gsum = sb("gsum", [P, 4, T * 2])
        wstack = sb("wstack", [P, T, KSTK], BF16)
        WT = sb("WT", [KSTK, C], BF16)
        prod = sb("prod", [P, 3, C])
        PH = sb("PH", [P, 2, C], F32R)
        PL = sb("PL", [P, 2, C], F32R)
        positions = sb("positions", [P, ST], I32)
        peak = sb("peak", [P, T, NH])
        peak_rest = sb("peak_rest", [P, T, NH])
        peak_part = sb("peak_part", [P, T, NG])
        peak_t = sb("peak_t", [P, T, 3 * NH], BF16)
        peak_f = sb("peak_f", [3 * NH, C], BF16)
        craw = sb("craw", [P, 2, C])
        cinv = sb("cinv", [P, 2, T, 4])
        logit_f = craw[:, 0, :]
        ctok = prod[:, 0:2, :].rearrange("p a b -> p (a b)").rearrange("p (t d) -> p t d", t=T)
        PS = ctx.enter_context(nc.psum_tensor("PS", [P, 8, 512], F32))

        parts_d = nc.dram_tensor("parts_d", (2, 3, D, C), BF16, kind="Internal").ap()
        peak_d = nc.dram_tensor("peak_d", (3 * NH, C), BF16, kind="Internal").ap()
        xr = x.rearrange("n (c t p) d -> n c p t d", c=NC, t=T)
        outr = out.rearrange("n (c t p) d -> n c p t d", c=NC, t=T)

        names = ("x_in0 x_in1 stat xn turned xhi xlo summed chi clo proj_kq part1 part_dve parts_out0 parts_out1 kq_in "
                 "projv v_in vs_in vs_zero keys_kept proj_r hidden logits logit_b gate_t gate_max gate_exp gates wt_t wt_in "
                 "xv_ps w_ps cum_ps xv_in xvw xvwc phi plo mixed scores peaks peak_parts peak_turned peak_copied "
                 "peak_out peak_in st exped masked av craw_in ctx_t ctx_rec ctx_tok ctx_f ctx_hi ctx_lo out_ps y stored0 stored1 rootd")
        front_names = ("x_in0 stat xn turned xhi xlo summed chi clo proj_kq part1 part_dve parts_out0 parts_out1 kq_in projv v_in "
                       "vs_in vs_zero keys_kept rootd")
        things = ("tok x_free x c_free c carry parts0 parts1 parts_d0 parts_d1 q kl kg va vs stats logit_f gate wstack wt peak "
                  "peak_t peak_f peak_d kept kq v v_shift xt0_in xt1_in xt0 xt1")
        pe, act, dve, pool, sp = (Queue() for _ in range(5))
        s = {n: tally("first_" + n) for n in front_names.split()}
        bank = [Latest(f"bank {i}") for i in range(8)]
        now = {n: Latest(n) for n in things.split()}
        rest_slot = [Latest(f"rest {i}") for i in range(2)]
        he_slot = [Latest(f"hidden/exp {i}") for i in range(4)]
        prod_slot = [Latest(f"product {i}") for i in range(3)]
        phl_slot = [Latest(f"split product {i}") for i in range(2)]
        craw_slot = [Latest(f"raw context {i}") for i in range(2)]

        def psum(i, rows=P, lo=0, hi=512):
            return PS[0:rows, i, lo:hi]

        def summed_mms(ps, pairs, tl):
            n = len(pairs)
            for k, (a, b) in enumerate(pairs):
                m = pe.do(lambda e, _, a=a, b=b, k=k: e.matmul(ps, a, b, start=(k == 0), stop=(k == n - 1), skip_group_check=True),
                          tl if k == n - 1 else None)
            return m

        def project(i, col, src_h, src_l, tl):
            pairs = []
            for k in range(DB):
                wh, wl = WH[:, k, col:col + P], WL[:, k, col:col + P]
                pairs += [(wh, src_h[:, k, :]), (wh, src_l[:, k, :]), (wl, src_h[:, k, :])]
            pe.wait_latest(bank[i])
            return summed_mms(psum(i), pairs, tl)

        def load_x(c, of):
            sp.wait_latest(now[f"xt{c}"])
            now[f"xt{c}_in"].marks = [sp.do(lambda e, n: e.dma_start(xt[c][:, :, :], xr[of(n), c]), s[f"x_in{c}"], 16, apart=True)]

        def normalise(c):
            X = xt[c]
            dve.wait_latest(now[f"xt{c}_in"])
            dve.wait_latest(now["stats"])
            for t in range(T):
                m = dve.do(lambda e, _, t=t: e.bn_stats(stats[:, t, :], X[:, t, :]), s["stat"])
            dve.wait(m)
            for t in range(T):
                m = dve.do(lambda e, _, t=t: e.bn_aggr(mv[:, t, :], stats[:, t, :]), s["stat"], apart=(t == 0))
            dve.wait(m)
            v, y0, a1, a2, y = (var[:, k, :] for k in (0, 1, 2, 3, 4))
            dve.wait(dve.do(lambda e, _: e.tensor_scalar(v, mv[:, :, 1], LN_EPS, None, ALU.add), s["stat"]))
            act.wait(dve.do(lambda e, _: e.reciprocal(a1, v), s["stat"]))
            m = act.do(lambda e, _: e.activation(y0, a1, ACT.Sqrt), s["rootd"])
            dve.wait(m)
            dve.wait(dve.do(lambda e, _: e.tensor_tensor(a2, y0, y0, ALU.mult), s["stat"]))
            dve.wait(dve.do(lambda e, _: e.tensor_tensor(a1, a2, v, ALU.mult), s["stat"]))
            dve.wait(dve.do(lambda e, _: e.tensor_scalar(a2, a1, -0.5, 1.5, ALU.mult, ALU.add), s["stat"]))
            dve.wait(dve.do(lambda e, _: e.tensor_tensor(y, a2, y0, ALU.mult), s["stat"]))
            dve.wait_latest(now["tok"])
            for t in range(T):
                m = dve.do(lambda e, _, t=t: e.tensor_scalar(tok[:, t, :], X[:, t, :], mv[:, t, 0:1], var[:, 4, t:t + 1],
                                                             ALU.subtract, ALU.mult), s["xn"])
            now["stats"].marks = [m]
            return m

        def turn_tokens(c, normalised):
            pe.wait(normalised)
            his, los, chis, clos = [], [], [], []
            for k in range(DB):
                i = 2 + k
                pe.wait_latest(bank[i])
                for t in range(T):
                    mt = pe.do(lambda e, _, t=t, k=k, i=i: e.transpose(psum(i, lo=t * P, hi=(t + 1) * P), tok[:, t, k * P:(k + 1) * P], ident[:, :]), s["turned"])
                act.wait(mt)
                if k == 0:
                    act.wait_latest(now["x_free"])
                his.append(act.do(lambda e, _, k=k, i=i: e.activation(XH[:, k, :], psum(i), ACT.Copy), s["xhi"]))
                dve.wait(his[-1])
                los.append(dve.do(lambda e, _, k=k, i=i: e.tensor_tensor(XL[:, k, :], psum(i), XH[:, k, :].bitcast(F32), ALU.subtract), s["xlo"]))
                dve.wait_latest(rest_slot[k])
                if c:
                    dve.wait_latest(now["carry"])
                init = carry[:, k:k + 1] if c else 0.0
                ms = dve.do(lambda e, _, k=k, i=i, init=init: e.tensor_tensor_scan(
                    rest[:, k, :], psum(i), XH[:, k, :].bitcast(F32), init, ALU.add, ALU.bypass), s["summed"])
                bank[i].marks = [ms]
                act.wait(ms)
                if k == 0:
                    act.wait_latest(now["c_free"])
                mch = act.do(lambda e, _, k=k: e.activation(CH[:, k, :], rest[:, k, :], ACT.Copy), s["chi"])
                pool.wait(mch)
                mcl = pool.do(lambda e, _, k=k: e.tensor_tensor(CL[:, k, :], rest[:, k, :], CH[:, k, :].bitcast(F32), ALU.subtract), s["clo"])
                rest_slot[k].marks = [mcl]
                if c == 0:
                    dve.wait(ms)
                    mc = dve.do(lambda e, _, k=k: e.tensor_copy(carry[:, k:k + 1], rest[:, k, C - 1:C]), s["summed"])
                    now["carry"].marks = [mc]
                    rest_slot[k].marks.append(mc)
            now["tok"].marks = [mt]
            now["x"].marks = [his[-1], los[-1]]
            now["c"].marks = [mch, mcl]

        def parts_block(w, b):
            col, bias = ((COL_K, k_bias) if w else (COL_Q, q_bias))
            i = r = b
            i += 2
            if b == 0:
                act.wait_latest(now[f"parts{w}"])
                dve.wait_latest(now[f"parts{w}"])
            pe.wait_latest(now["x"])
            m = project(i, col + b * P, XH, XL, s["proj_kq"])
            p1, p2, p3 = (parts[:, w, j, b, :] for j in range(3))
            left = rest[:, r, :]
            act.wait(m)
            m1 = act.do(lambda e, _: e.activation(p1, psum(i), ACT.Identity, bias=bias[:, b:b + 1]), s["part1"])
            dve.wait(m1)
            dve.wait_latest(rest_slot[r])
            m2 = dve.do(lambda e, _: e.scalar_tensor_tensor(out=left, in0=psum(i), scalar=bias[:, b:b + 1], in1=p1,
                                                            op0=ALU.add, op1=ALU.subtract), s["part_dve"])
            bank[i].marks = [m2]
            dve.wait(m2)
            m3 = dve.do(lambda e, _: e.tensor_copy(p2, left), s["part_dve"])
            dve.wait(m3)
            m4 = dve.do(lambda e, _: e.tensor_tensor(p3, left, p2, ALU.subtract), s["part_dve"])
            rest_slot[r].marks = [m4]
            if b == DB - 1:
                sp.wait(m1, m4)
                sp.wait_latest(now[f"parts_d{w}"])
                mo = sp.do(lambda e, _: e.dma_start(parts_d[w].rearrange("i (b p) t -> p i b t", p=P), parts[:, w, :, :, :]), s[f"parts_out{w}"], 16)
                now[f"parts{w}"].marks = [mo]

        def keep_keys(c):
            dve.wait_latest(now["kl"])
            if c == 0:
                mk = dve.do(lambda e, _: e.memset(KL[0:KSTK, :, 0:WINDOW], 0.0), s["keys_kept"])
            else:
                mk = dve.do(lambda e, _: e.tensor_copy(KL[0:KSTK, :, 0:WINDOW], KL[0:KSTK, :, C:C + WINDOW]), s["keys_kept"])
            now["kept"].marks = [mk]

        def load_stacks(c):
            sp.wait_latest(now["kept"])
            for w in (1, 0):
                sp.wait_latest(now[f"parts{w}"])
                for n in ("kl", "kg") if w else ("q",):
                    sp.wait_latest(now[n])
                for g in range(6):
                    rows = slice(HD * g, HD * (g + 1))
                    src = parts_d[w, (LEFT if w else RIGHT)[g]].rearrange("(h d) t -> d h t", d=HD)
                    if w:
                        sp.do(lambda e, _, rows=rows, src=src: e.dma_start(KL[rows, :, WINDOW:], src[:, NG:, :]), s["kq_in"], 16)
                        mi = sp.do(lambda e, _, rows=rows, src=src: e.dma_start(KG[rows, :, c * C:(c + 1) * C], src[:, 0:NG, :]), s["kq_in"], 16)
                    else:
                        mi = sp.do(lambda e, _, rows=rows, src=src: e.dma_start(QS[rows, :, :], src), s["kq_in"], 16)
                now[f"parts_d{w}"].marks = [mi]
            now["parts_d1"].marks = [mi]
            now["kq"].marks = [mi]

        def values(c):
            pe.wait_latest(now["x"])
            act.wait_latest(now["va"])
            for u in range(T // 2):
                i = 2 + u
                pe.wait_latest(bank[i])
                for a in range(2):
                    t = 2 * u + a
                    pairs = []
                    for k in range(DB):
                        wh, wl = WH[:, k, COL_V:COL_V + D], WL[:, k, COL_V:COL_V + D]
                        xh, xl = XH[:, k, t * P:(t + 1) * P], XL[:, k, t * P:(t + 1) * P]
                        pairs += [(xh, wh), (xh, wl), (xl, wh)]
                    m = summed_mms(psum(i, lo=a * D, hi=(a + 1) * D), pairs, s["projv"])
                act.wait(m)
                tt = c * T + 2 * u
                mv_ = act.do(lambda e, _, i=i, tt=tt: e.activation(
                    Va[:, tt:tt + 2, :, 0:HD], psum(i).rearrange("p (a h d) -> p a h d", a=2, h=NH), ACT.Copy), s["v_in"])
                bank[i].marks = [mv_]
            now["v"].marks = [mv_]
            sp.wait(mv_)
            sp.wait_latest(now["vs"])
            t0 = c * T
            now["v_shift"].marks = []
            if c == 0:
                pool.wait_latest(now["vs"])
                now["v_shift"].marks = [pool.do(lambda e, _: e.memset(Vs[0:WINDOW, 0, :, :], 0.0), s["vs_zero"], apart=True)]
                sp.do(lambda e, _: e.dma_start(Vs[0:WINDOW, 1:T, :, :], Va[WINDOW:P, 0:T - 1, NG:, :]), s["vs_in"], 16)
            else:
                sp.do(lambda e, _: e.dma_start(Vs[0:WINDOW, :, :, :], Va[WINDOW:P, t0 - 1:t0 + T - 1, NG:, :]), s["vs_in"], 16)
            now["v_shift"].marks.append(sp.do(lambda e, _: e.dma_start(Vs[WINDOW:P, :, :, :], Va[0:WINDOW, t0:t0 + T, NG:, :]), s["vs_in"], 16))

        s_raw = [tally(f"raw_loaded{i}") for i in range(4)]
        s_pe0 = tally("setup_pe")
        s_act0 = tally("setup_act")
        s_dve0 = tally("setup_dve")
        s_pool0 = tally("setup_pool")
        s_put0 = tally("setup_rows_put")
        at[0] = 0

        def raw(shape):
            n = shape[0] * shape[1]
            return carve(n).rearrange("p (a b) -> p a b", a=shape[0])

        rQKV = raw((DB, 3 * D))
        rWQ, rWK, rWI, rWO, rR1, tWI, tWO, tR1, rOUT = (raw((DB, D)) for _ in range(9))
        gQ, gK = rWI, rR1
        rV = [raw((DB, KR)) for _ in range(4)]
        rU = [raw((DB, KR)) for _ in range(2)]
        assert at[0] <= AREA
        rows8 = HE[0:KE, 0, :]
        rows8b = HE[0:KE, 1, :]
        columns = HE[:, 2, 0:64]
        borow = HE[0:1, 2, 256:256 + D]
        alpha1 = HE[0:1, 3, 0:1]
        ones1 = HE[0:1, 3, 8:8 + P]
        alphac = HE[:, 3, 200:201]
        brow = [prod[0:KE, 0, 0:D], prod[0:KE, 0, D:2 * D], prod[0:1, 1, 0:D]]
        brest = [[xt[1][0:KE, k, :] for k in (0, 1)], [xt[1][0:KE, k, :] for k in (2, 3)],
                 [prod[0:1, 1, D:2 * D], prod[0:1, 2, 0:D]]]
        bpart = [[craw[0:KE, j, D * i // 2:D * (i + 1) // 2].bitcast(BF16) for i in range(3)] for j in range(2)] + \
                [[WT[0:1, 0:D], WT[0:1, D:2 * D], peak_f[0:1, 0:D]]]

        def load(dst, src, group):
            return sp.do(lambda e, _: e.dma_start(dst, src), s_raw[group], 16)

        for view in (l_bias[:, :], rows8b[:, D:D + P]):
            blank = dve.do(lambda e, _, view=view: e.memset(view, 0.0), s_dve0)
        load_x(0, lambda n: 0)
        sp.wait(blank)
        load(rows8b[:, 0:D], b_inv, 0)
        load(rows8[:, 0:D], router_w2, 0)
        load(rows8[:, D:2 * D], b_fwd, 0)
        load(rows8b[0:6, D:D + P], b_qkv.rearrange("(a b) -> a b", b=P), 0)
        load(rows8b[6:8, D:D + P], router_b1.rearrange("(a b) -> a b", b=P), 0)
        load(borow, b_out.rearrange("(a d) -> a d", a=1), 0)
        load(alpha1, alpha.rearrange("(a d) -> a d", a=1), 0)
        for w in range(2):
            l_at = slice(64 * w, 64 * w + KE)
            load(l_bias[l_at, 0:1], router_b2.rearrange("(k a) -> k a", a=1), 0)
            load_0 = load(l_bias[l_at, 1:2], expert_bias.rearrange("(k a) -> k a", a=1), 0)
        for dst, src in ((rWI, W_inv), (rWQ, W_Q), (rWK, W_K), (rR1, router_w1), (rWO, W_O)):
            load_1 = load(dst, src.rearrange("(b p) d -> p b d", p=P), 1)
        for dst, src in zip(rV, (V_fwd, W_inv_exp, W_fwd, V_inv)):
            for b in range(DB):
                load_2 = load(dst[:, b, :].rearrange("p (k r) -> p k r", k=KE), src[:, b * P:(b + 1) * P, :].rearrange("k p r -> p k r"), 2)
        load(rQKV, w_qkv.rearrange("(b p) d -> p b d", p=P), 3)
        load(rOUT, w_out.rearrange("(b p) d -> p b d", p=P), 3)
        for dst, src in zip(rU, (U_fwd, U_inv)):
            for b in range(DB):
                load_3 = load(dst[:, b, :].rearrange("p (k r) -> p k r", k=KE), src[:, b * P:(b + 1) * P, :].rearrange("k p r -> p k r"), 3)

        for view, value in ((ident[:, :], 0.0), (ident_b[:, :], 0.0), (band[:, :, :], 0.0), (strip[:, :], 0.0),
                            (spread[:, :, :], 0.0)):
            cleared = dve.do(lambda e, _, view=view, value=value: e.memset(view, value), s_dve0)
        pool.wait(cleared)

        def select(view, pattern, base, cm, op=ALU.is_ge, fill=MASKED):
            m = pool.do(lambda e, _: e.affine_select(out=view, in_=view, compare_op=op, fill=fill, base=base,
                                                     pattern=pattern, channel_multiplier=cm), s_pool0)
            pool.wait(m)
            return m

        for view in (ident[:, :], ident_b[:, :]):
            ident_in = select(view, [[1, P]], 0, -1, ALU.not_equal, 1.0)
        BW = P + WINDOW
        for v in range(2):
            select(band[:, v, :], [[1, BW]], 0, -1)
            select(band[:, v, :], [[-1, BW]], WINDOW, 1)
        select(band[:, 1, :], [[1, BW]], -WINDOW, 0)
        select(strip[:, :], [[-1, C]], C - P, 1)
        for first in (0, 3 * HD, 5 * HD):
            view = spread[:, :, :].rearrange("r j (a m) -> r (j a) m", a=2)
            select(view, [[-1, 4 * KB], [0, R]], -first, 1, ALU.not_equal, 1.0)
        count = positions[:, :]
        counted = pool.do(lambda e, _: e.iota(count, pattern=[[P, ST]], base=1, channel_multiplier=1), s_pool0)

        pe.wait(ident_in)
        normalised0 = normalise(0)
        turn_tokens(0, normalised0)

        for view, value in ((ones1, 1.0), (wstack[:, :, :], 1.0), (Va[:, :, :, :], 1.0),
                            (craw[:, :, :], 0.0)):
            cleared = dve.do(lambda e, _, view=view, value=value: e.memset(view, value), s_dve0)
        dve.wait(counted)
        dve.wait(dve.do(lambda e, _: e.tensor_copy(inv_n[:, :], count), s_dve0))
        dve.wait(dve.do(lambda e, _: e.reciprocal(inv_n[:, :], inv_n[:, :]), s_dve0))
        for i in (4, 7):
            cleared = dve.do(lambda e, _, i=i: e.memset(PS[:, i, :], 0.0), s_dve0)
            bank[i].marks = [cleared]
        dve.wait(load_0)
        for w in range(2):
            l_at = slice(64 * w, 64 * w + KE)
            dve.do(lambda e, _, l_at=l_at: e.tensor_tensor(l_bias[l_at, 0:1], l_bias[l_at, 0:1], l_bias[l_at, 1:2], ALU.add), s_dve0)
        bank_of = [0]

        def next_bank():
            i = bank_of[0] % 8
            bank_of[0] += 1
            pe.wait_latest(bank[i])
            return i

        def product(rows, lhsTs, rhss, n):
            i = next_bank()
            for k, (a, b) in enumerate(zip(lhsTs, rhss)):
                m = pe.do(lambda e, _, a=a, b=b, k=k: e.matmul(PS[0:rows, i, 0:n], a, b, start=(k == 0), stop=(k == len(lhsTs) - 1)), s_pe0)
            return i, m

        def put_split(hi, lo, src, ready, scale=None):
            act.wait(ready)
            if scale is None:
                h = act.do(lambda e, _: e.activation(hi, src, ACT.Copy), s_act0)
                dve.wait(h)
                return dve.do(lambda e, _: e.tensor_tensor(lo, src, hi.bitcast(F32), ALU.subtract), s_dve0)
            h = act.do(lambda e, _: e.activation(hi, src, ACT.Identity, scale=scale), s_act0)
            dve.wait(h)
            return dve.do(lambda e, _: e.scalar_tensor_tensor(out=lo, in0=src, scalar=scale, in1=hi.bitcast(F32),
                                                              op0=ALU.mult, op1=ALU.subtract), s_dve0)

        pe.wait(load_0)
        act.wait(load_0)
        i = next_bank()
        for k, src in enumerate([rows8[:, b * P:(b + 1) * P] for b in range(4)] + [rows8b[:, b * P:(b + 1) * P] for b in range(3)]):
            m = pe.do(lambda e, _, k=k, src=src, i=i: e.transpose(PS[:, i, k * KE:(k + 1) * KE], src, ident[0:KE, 0:KE]), s_pe0)
        act.wait(m)
        m = act.do(lambda e, _, i=i: e.activation(columns[:, 0:7 * KE], PS[:, i, 0:7 * KE], ACT.Copy), s_act0)
        bank[i].marks = [m]
        act.wait(m)
        pe.wait(m)
        column = lambda k: columns[:, k * KE:(k + 1) * KE]
        act.do(lambda e, _: e.activation(W2[:, :, :].rearrange("p b k -> p (b k)"), columns[:, 0:2 * KE], ACT.Copy), s_act0)
        for dst, k in ((q_bias, 0), (k_bias, 2), (r_bias, 6)):
            m = act.do(lambda e, _, dst=dst, k=k: e.activation(dst[:, :], column(6)[:, k:k + 2], ACT.Copy), s_act0)
        braw = [[column(2), column(3)], [column(4), column(5)]]
        bvraw = column(6)[:, 4:6]
        pe.wait(cleared)
        i, m = product(P, [ones1], [alpha1], 1)
        dve.wait(m)
        alpha_in = dve.do(lambda e, _, i=i: e.tensor_copy(alphac, PS[:, i, 0:1]), s_dve0)
        bank[i].marks = [alpha_in]
        pe.wait(load_1)
        turned = []
        for src, dst in ((rWI, tWI), (rR1, tR1), (rWO, tWO)):
            for b in range(DB):
                i = next_bank()
                for a in range(DB):
                    m = pe.do(lambda e, _, a=a, b=b, i=i, src=src: e.transpose(PS[:, i, a * P:(a + 1) * P], src[:, a, b * P:(b + 1) * P], ident[:, :]), s_pe0)
                act.wait(m)
                turned.append(act.do(lambda e, _, b=b, i=i, dst=dst: e.activation(dst[:, b, :], PS[:, i, 0:D], ACT.Copy), s_act0))
                bank[i].marks = [turned[-1]]
        pe.wait(*turned)
        joined = []
        for src, dst in ((rWQ, gQ), (rWK, gK)):
            for f in range(DB):
                i, m = product(P, [tWI[:, e_, f * P:(f + 1) * P] for e_ in range(DB)], [src[:, e_, :] for e_ in range(DB)], D)
                act.wait(m)
                joined.append(act.do(lambda e, _, f=f, i=i, dst=dst: e.activation(dst[:, f, :], PS[:, i, 0:D], ACT.Copy), s_act0))
                bank[i].marks = [joined[-1]]
        act.wait(alpha_in)
        dve.wait(alpha_in)
        pe.wait(load_2)
        for left, right, col, n in ((rWQ, rV[0], COL_X, KR), (rWK, rV[2], COL_C, KR), (rWQ, tR1, COL_R, D), (gQ, tR1, COL_R + D, D),
                                    (gQ, rV[1], COL_X + KR, KR), (gK, rV[3], COL_C + KR, KR)):
            if left is gQ or left is gK:
                pe.wait(*joined)
            for d in range(DB):
                i, m = product(P, [left[:, e_, d * P:(d + 1) * P] for e_ in range(DB)], [right[:, e_, :] for e_ in range(DB)], n)
                bank[i].marks = [put_split(WH[:, d, col:col + n], WL[:, d, col:col + n], PS[:, i, 0:n], m)]
        pe.wait(load_3)
        put_split(OH[:, :, :], OL[:, :, :], rOUT, load_3)
        qkv_in = put_split(WH[:, :, 0:3 * D], WL[:, :, 0:3 * D], rQKV, load_3)
        made = []
        for w in range(2):
            i, m = product(KE, braw[w], [tWO[:, e_, :] for e_ in range(DB)], D)
            dve.wait(m)
            made.append(dve.do(lambda e, _, i=i, w=w: e.tensor_scalar(brow[w], PS[0:KE, i, 0:D], alphac[0:KE, :] if w else 1.0, None, ALU.mult), s_dve0))
            bank[i].marks = [made[-1]]
        i, m = product(1, [bvraw[:, e_:e_ + 1] for e_ in range(DB)], [rOUT[:, e_, :] for e_ in range(DB)], D)
        dve.wait(m)
        made.append(dve.do(lambda e, _, i=i: e.tensor_tensor(brow[2], PS[0:1, i, 0:D], borow, ALU.add), s_dve0))
        bank[i].marks = [made[-1]]
        dve.wait(*made)
        for w in range(3):
            src = brow[w]
            for p in range(3):
                m = dve.do(lambda e, _, w=w, p=p, src=src: e.tensor_copy(bpart[w][p], src), s_dve0)
                dve.wait(m)
                if p < 2:
                    m2 = dve.do(lambda e, _, w=w, p=p, src=src: e.tensor_tensor(brest[w][p], src, bpart[w][p], ALU.subtract), s_dve0)
                    dve.wait(m2)
                    src = brest[w][p]
        sp.wait(m)
        for g in range(6):
            for w in range(2):
                sp.do(lambda e, _, g=g, w=w: e.dma_start(bias_rows[HD * g + KE * w:HD * g + KE * (w + 1), :], bpart[w][RIGHT[g]]), s_put0, 16)
        for p in range(3):
            put = sp.do(lambda e, _, p=p: e.dma_start(bias_rows[G16 + p:G16 + p + 1, :], bpart[2][p]), s_put0, 16)
        for w in range(2):
            for j in range(KB):
                i, m = product(P, [rU[w][:, e_, j * P:(j + 1) * P] for e_ in range(DB)], [tWO[:, e_, :] for e_ in range(DB)], D)
                bank[i].marks = [put_split(UH[:, KB * w + j, :], UL[:, KB * w + j, :], PS[:, i, 0:D], m,
                                           scale=alphac if w else None)]
        last_pe, last_act, last_dve = (Mark(t_, t_.n) for t_ in (s_pe0, s_act0, s_dve0))
        for q_ in (pe, act, dve, pool, sp):
            q_.wait(last_pe, last_act, last_dve)
        dve.do(lambda e, _: e.memset(KG[G16:KSTK, :, :], 1.0), s_dve0)
        ones_in = dve.do(lambda e, _: e.memset(KL[G16:KSTK, :, :], 1.0), s_dve0)
        dve.wait(ones_in)
        for w in (1, 0):
            for b in range(DB):
                parts_block(w, b)
        keep_keys(0)
        load_stacks(0)
        values(0)
        sp.wait(put)
        for n in ("kq", "v_shift"):
            sp.wait_latest(now[n])
        setup = (pe, act, dve, pool, sp)
        with nc.Block() as block:
            block.tensor(lambda e: setup[0].write(e))
            block.scalar(lambda e: setup[1].write(e))
            block.vector(lambda e: setup[2].write(e))
            block.gpsimd(lambda e: setup[3].write(e))
            block.sync(lambda e: setup[4].write(e))

        pe, act, dve, pool, sp = (Queue() for _ in range(5))
        s = {n: tally(n) for n in names.split()}
        for thing in [*bank, *now.values(), *rest_slot, *he_slot, *prod_slot, *phl_slot, *craw_slot]:
            thing.marks = []

        def router_hidden(c):
            pe.wait_latest(now["x"])
            hs = []
            for j in range(2 * DB):
                i = (2, 3, 4, 7)[j]
                m = project(i, COL_R + j * P, XH, XL, s["proj_r"])
                act.wait(m)
                act.wait_latest(he_slot[j])
                hs.append(act.do(lambda e, _, i=i, j=j: e.activation(HE[:, j, :], psum(i), ACT.Gelu, bias=r_bias[:, j % DB:j % DB + 1]), s["hidden"]))
                bank[i].marks = [hs[-1]]
            return hs

        def router_logits(c, hs):
            pe.wait(*hs)
            pe.wait_latest(bank[7])
            for j in range(2 * DB):
                m = pe.do(lambda e, _, j=j: e.matmul(PS[32 * j:32 * j + KE, 7, :], W2[:, j % DB, :], HE[:, j, :], start=True, stop=True,
                                                     skip_group_check=True), s["logits"])
                he_slot[j].marks = [m]
            act.wait(m)
            act.wait_latest(craw_slot[0])
            ml = act.do(lambda e, _: e.activation(logit_f, psum(7), ACT.Identity, bias=l_bias[:, 0:1]), s["logit_b"])
            bank[7].marks = [ml]
            return ml

        def router_weights(c, ml):
            pe.wait(ml)
            pe.wait_latest(bank[7])
            for t in range(T):
                m = pe.do(lambda e, _, t=t: e.transpose(psum(7, lo=t * P, hi=(t + 1) * P), logit_f[:, t * P:(t + 1) * P],
                                                        ident[:, :]), s["gate_t"])
            craw_slot[0].marks = [m]
            lg = psum(7).rearrange("p (t w a k) -> p t w a k", t=T, w=2, a=2)[:, :, :, :, 0:KE]
            g4 = [gate[:, k, :, :].rearrange("p t (w k) -> p (t w) k", k=KE) for k in range(4)]
            g5 = [gate[:, k, :, :].rearrange("p t (w k) -> p t w k", k=KE) for k in range(4)]
            dve.wait(m)
            dve.wait_latest(now["gate"])
            dve.wait(dve.do(lambda e, _: e.tensor_copy(g5[0], lg[:, :, :, 0, :]), s["gate_max"]))
            m = dve.do(lambda e, _: e.tensor_tensor(g5[3], lg[:, :, :, 1, :], g5[0], ALU.add), s["gate_max"])
            bank[7].marks = [m]
            dve.wait(m)
            dve.wait(dve.do(lambda e, _: e.tensor_reduce(gsum[:, 0, :], g4[3], AX_X, ALU.max), s["gate_max"]))
            m = dve.do(lambda e, _: e.tensor_tensor(g4[0], g4[3], gsum[:, 0, :].unsqueeze(2).to_broadcast([P, 2 * T, KE]), ALU.subtract), s["gate_max"])
            act.wait(m)
            m = act.do(lambda e, _: e.activation(g4[1], g4[0], ACT.Exp), s["gate_exp"])
            dve.wait(m)
            dve.wait(dve.do(lambda e, _: e.tensor_reduce(gsum[:, 1, :], g4[1], AX_X, ALU.add), s["gates"]))
            dve.wait(dve.do(lambda e, _: e.reciprocal(gsum[:, 2, :], gsum[:, 1, :]), s["gates"]))
            dve.wait(dve.do(lambda e, _: e.tensor_tensor(
                gsum[:, 3, :].rearrange("p (t w) -> p t w", w=2), gsum[:, 2, :].rearrange("p (t w) -> p t w", w=2),
                inv_n[:, c * T:(c + 1) * T].unsqueeze(2).to_broadcast([P, T, 2]), ALU.mult), s["gates"]))
            dve.wait(dve.do(lambda e, _: e.tensor_tensor(g4[2], g4[1], gsum[:, 3, :].unsqueeze(2).to_broadcast([P, 2 * T, KE]), ALU.mult), s["gates"]))
            dve.wait_latest(now["wstack"])
            ws = wstack[:, :, 0:G16].rearrange("p t (g k) -> p t g k", k=2 * KE)
            w_f, w_r = gate[:, 2], gate[:, 3]

            def copies(src, n):
                return src.unsqueeze(2).to_broadcast([P, T, n, 2 * KE])

            dve.wait(dve.do(lambda e, _: e.tensor_copy(ws[:, :, 0:3, :], copies(w_f, 3)), s["gates"]))
            dve.wait(dve.do(lambda e, _: e.tensor_tensor(w_r, w_f, ws[:, :, 0, :], ALU.subtract), s["gates"]))
            dve.wait(dve.do(lambda e, _: e.tensor_copy(ws[:, :, 3:5, :], copies(w_r, 2)), s["gates"]))
            m = dve.do(lambda e, _: e.tensor_tensor(ws[:, :, 5, :], w_r, ws[:, :, 3, :], ALU.subtract), s["gates"])
            now["gate"].marks = [m]
            return m

        def router_rows(c, m):
            pe.wait(m)
            pe.wait_latest(bank[7])
            wt_ps = PS[0:KSTK, 7, :].bitcast(BF16)
            for t in range(T):
                m = pe.do(lambda e, _, t=t: e.transpose(wt_ps[:, t * P:(t + 1) * P], wstack[:, t, :], ident_b[:, :]), s["wt_t"])
            now["wstack"].marks = [m]
            act.wait(m)
            act.wait_latest(now["wt"])
            m = act.do(lambda e, _: e.activation(WT[:, :], wt_ps[:, 0:C], ACT.Copy), s["wt_in"])
            bank[7].marks = [m]
            return m

        def out_ps(t):
            return psum(t // 2, lo=(t % 2) * D, hi=(t % 2 + 1) * D)

        def open_out(c, rows_in):
            pe.wait(rows_in)
            for t in range(T):
                if t % 2 == 0:
                    pe.wait_latest(bank[t // 2])
                pe.do(lambda e, _, t=t: e.matmul(out_ps(t), WT[:, t * P:(t + 1) * P], bias_rows[:, :], start=(t % 2 == 0), stop=False,
                                                 skip_group_check=True))

        halves = {}

        def expert_x(c, j):
            r = j % 3
            m_x = project(2, COL_X + j * P, XH, XL, s["xv_ps"])
            act.wait(m_x)
            act.wait_latest(prod_slot[r])
            m = act.do(lambda e, _: e.activation(prod[:, r, :], psum(2), ACT.Copy), s["xv_in"])
            bank[2].marks = [m]
            halves["x"] = m
            if j == 2 * KB - 1:
                now["x_free"].marks = [m_x, Mark(s["projv"], s["projv"].n)] if s["projv"].n else [m_x]

        def expert_c(c, j, rows_in):
            r, h = j % 3, j % 2
            if j == 0:
                pe.wait_latest(now["c"])
            m_c = project(3, COL_C + j * P, CH, CL, s["cum_ps"])
            pe.wait(rows_in)
            pe.wait_latest(bank[4])
            m_w = pe.do(lambda e, _: e.matmul(psum(4), spread[:, j, :], WT[:, :], start=True, stop=True), s["w_ps"])
            dve.wait(halves["x"], m_w)
            m = dve.do(lambda e, _: e.tensor_tensor(prod[:, r, :], psum(4), prod[:, r, :], ALU.mult), s["xvw"])
            bank[4].marks = [m]
            dve.wait(m, m_c)
            m = dve.do(lambda e, _: e.tensor_tensor(prod[:, r, :], psum(3), prod[:, r, :], ALU.mult), s["xvwc"])
            bank[3].marks = [m]
            act.wait(m)
            act.wait_latest(phl_slot[h])
            mh = act.do(lambda e, _: e.activation(PH[:, h, :], prod[:, r, :], ACT.Copy), s["phi"])
            pool.wait(mh)
            ml = pool.do(lambda e, _: e.tensor_tensor(PL[:, h, :], prod[:, r, :], PH[:, h, :].bitcast(F32), ALU.subtract), s["plo"])
            prod_slot[r].marks = [ml]
            halves["p", j] = (mh, ml)
            if j == 2 * KB - 1:
                now["wt"].marks = [m_w]
                now["c_free"].marks = [m_c]

        def mix(c, j):
            h = j % 2
            mh, ml = halves["p", j]
            pe.wait(mh)
            for part, uu in ((PH, (UH, UL)), (PL, (UH,))):
                if part is PL:
                    pe.wait(ml)
                for t in range(T):
                    for u in uu:
                        m = pe.do(lambda e, _, t=t, part=part, u=u: e.matmul(
                            out_ps(t), part[:, h, t * P:(t + 1) * P], u[:, j, :], start=False, stop=False, skip_group_check=True), s["mixed"])
            phl_slot[h].marks = [m]

        turns = {"score": 0, "exp": 0}

        def score_bank():
            turns["score"] ^= 1
            return 5 + turns["score"]

        def peaks_local(c, t, pair):
            i = score_bank()
            if t == 0 and pair == 0:
                pe.wait_latest(now["kq"])
                pe.wait_latest(now["kept"])
                dve.wait_latest(now["peak"])
            pe.wait_latest(bank[i])
            for a in range(2):
                l = 2 * pair + a
                m = pe.do(lambda e, _, a=a, l=l: e.matmul(psum(i, lo=256 * a, hi=256 * a + BW), QS[0:G16, NG + l, t * P:(t + 1) * P],
                                                          KL[0:G16, l, t * P:t * P + BW], start=(a == 0), stop=(a == 1),
                                                          skip_group_check=True), s["scores"])
            dve.wait(m)
            which = 1 if c == 0 and t == 0 else 0
            for a in range(2):
                h = NG + 2 * pair + a
                ps = psum(i, lo=256 * a, hi=256 * a + BW)
                m = dve.do(lambda e, _, ps=ps, h=h: e.tensor_tensor_reduce(
                    ps, ps, band[:, which, :], 1.0, LOWEST, ALU.add, ALU.max, peak[:, t, h:h + 1]), s["peaks"], apart=(a == 0))
            bank[i].marks = [m]
            return m

        def peaks_global(c, t, g):
            start = LOWEST
            for q in range(c + 1):
                i = score_bank()
                n = C if q < c else (t + 1) * P
                pe.wait_latest(bank[i])
                m = pe.do(lambda e, _, q=q, n=n, i=i: e.matmul(psum(i, hi=n), QS[0:G16, g, t * P:(t + 1) * P], KG[0:G16, g, q * C:q * C + n],
                                                               start=True, stop=True), s["scores"])
                dve.wait(m)
                if q < c:
                    m = dve.do(lambda e, _, i=i: e.tensor_reduce(peak_part[:, t, g:g + 1], psum(i), AX_X, ALU.max), s["peak_parts"])
                    bank[i].marks = [m]
                    dve.wait(m)
                    start = peak_part[:, t, g:g + 1]
                else:
                    m = dve.do(lambda e, _, n=n, i=i, start=start: e.tensor_tensor_reduce(
                        psum(i, hi=n), psum(i, hi=n), strip[:, C - n:C], 1.0, start, ALU.add, ALU.max, peak[:, t, g:g + 1]), s["peaks"], apart=True)
                    bank[i].marks = [m]
            return m

        def peaks_to_rows(c, found):
            pt = [peak_t[:, :, k * NH:(k + 1) * NH] for k in range(3)]
            dve.wait(found)
            dve.wait_latest(now["peak_t"])
            dve.wait(dve.do(lambda e, _: e.tensor_scalar(pt[0], peak[:, :, :], -1.0, None, ALU.mult), s["peak_parts"]))
            dve.wait(dve.do(lambda e, _: e.scalar_tensor_tensor(out=peak_rest[:, :, :], in0=peak[:, :, :], scalar=-1.0, in1=pt[0],
                                                                op0=ALU.mult, op1=ALU.subtract), s["peak_parts"]))
            dve.wait(dve.do(lambda e, _: e.tensor_copy(pt[1], peak_rest[:, :, :]), s["peak_parts"]))
            m = dve.do(lambda e, _: e.tensor_tensor(pt[2], peak_rest[:, :, :], pt[1], ALU.subtract), s["peak_parts"])
            now["peak"].marks = [m]
            pe.wait(m)
            pe.wait_latest(bank[7])
            ps = PS[0:3 * NH, 7, :].bitcast(BF16)
            for t in range(T):
                m = pe.do(lambda e, _, t=t: e.transpose(ps[:, t * P:(t + 1) * P], peak_t[:, t, :], ident_b[:, :]), s["peak_turned"], apart=(t == 0))
            now["peak_t"].marks = [m]
            act.wait(m)
            act.wait_latest(now["peak_f"])
            m = act.do(lambda e, _: e.activation(peak_f[:, :], ps[:, 0:C], ACT.Copy), s["peak_copied"])
            bank[7].marks = [m]
            sp.wait(m)
            sp.wait_latest(now["peak_d"])
            m = sp.do(lambda e, _: e.dma_start(peak_d, peak_f[:, :]), s["peak_out"], 16)
            now["peak_f"].marks = [m]
            sp.wait(m)
            m = sp.do(lambda e, _: e.dma_start(QS[G16:KSTK, :, :], peak_d.rearrange("(a h) t -> a h t", h=NH)), s["peak_in"], 16)
            now["peak_d"].marks = [m]
            return m

        def exp_slot():
            turns["exp"] = (turns["exp"] + 1) % 4
            return turns["exp"]

        def attend_local(c, grp, half, peak_in):
            cb = 7 if grp % 2 else 4
            slots, ready = [], []
            for pair in range(2):
                i, k = score_bank(), exp_slot()
                slots.append(k)
                pe.wait(peak_in)
                pe.wait_latest(bank[i])
                for a in range(2):
                    l = 4 * (grp - 1) + 2 * pair + a
                    for w in range(4):
                        at_ = (4 * half + w) * WINDOW
                        m = pe.do(lambda e, _, a=a, l=l, w=w, at_=at_, i=i: e.matmul(
                            psum(i, lo=(4 * a + w) * WINDOW, hi=(4 * a + w + 1) * WINDOW), KL[0:KSTK, l, at_:at_ + P],
                            QS[0:KSTK, NG + l, at_:at_ + WINDOW], start=(a + w == 0), stop=(a == 1 and w == 3), skip_group_check=True), s["st"])
                act.wait(m)
                act.wait_latest(he_slot[k])
                m = act.do(lambda e, _, i=i, k=k: e.activation(HE[:, k, :], psum(i), ACT.Exp, scale=SCALE), s["exped"])
                bank[i].marks = [m]
                ev = HE[:, k, :].rearrange("p (w q) -> p w q", w=8)
                for pattern, base, cm in (([[0, 8], [-1, WINDOW]], 0, 1), ([[0, 8], [1, WINDOW]], WINDOW, -1)):
                    pool.wait(m)
                    m = pool.do(lambda e, _, pattern=pattern, base=base, cm=cm, ev=ev: e.affine_select(
                        out=ev, in_=ev, compare_op=ALU.is_ge, fill=0.0, base=base, pattern=pattern, channel_multiplier=cm), s["masked"], apart=True)
                ready.append(m)

            def av():
                if grp == 1 and half == 0:
                    pe.wait_latest(now["v"])
                    pe.wait_latest(now["v_shift"])
                pe.wait(*ready)
                if half == 0:
                    pe.wait_latest(bank[cb])
                for w in range(4):
                    for g in range(4):
                        l = 4 * (grp - 1) + g
                        t_, odd = c * T + 2 * half + w // 2, w % 2
                        v = Va[:, t_, NG + l, :] if odd else Vs[:, 2 * half + w // 2, l, :]
                        q = slice((4 * half + w) * WINDOW, (4 * half + w + 1) * WINDOW)
                        e_at = slice((4 * (g % 2) + w) * WINDOW, (4 * (g % 2) + w + 1) * WINDOW)
                        m2 = pe.do(lambda e, _, v=v, q=q, g=g, e_at=e_at, first=(half == 0 and w == 0): e.matmul(
                            PS[32 * g:32 * g + VW, cb, q], v, HE[:, slots[g // 2], e_at], start=first, stop=True,
                            skip_group_check=True), s["av"])
                for k in slots:
                    he_slot[k].marks = [m2]
                return m2, cb
            return av

        def attend_global(c, j, half, peak_in):
            HALF = C // 2
            lo = max(0, (j - c * T) * P - half * HALF)
            n = HALF - lo
            q = slice(half * HALF + lo, (half + 1) * HALF)
            diag = (j - c * T) * P >= half * HALF
            slots, ready = [], []
            for pair in range(2):
                i, k = score_bank(), exp_slot()
                slots.append(k)
                pe.wait(peak_in)
                pe.wait_latest(bank[i])
                for a in range(2):
                    g = 2 * pair + a
                    m = pe.do(lambda e, _, a=a, g=g, i=i: e.matmul(psum(i, lo=HALF * a + lo, hi=HALF * (a + 1)), KG[0:KSTK, g, j * P:(j + 1) * P],
                                                                   QS[0:KSTK, g, q], start=(a == 0), stop=(a == 1), skip_group_check=True), s["st"])
                act.wait(m)
                act.wait_latest(he_slot[k])
                two = lambda ap: ap.rearrange("p (a q) -> p a q", a=2)[:, :, lo:]
                m = act.do(lambda e, _, i=i, k=k: e.activation(two(HE[:, k, :]), two(psum(i)), ACT.Exp, scale=SCALE), s["exped"])
                bank[i].marks = [m]
                if diag:
                    pool.wait(m)
                    ev = HE[:, k, :].rearrange("p (a q) -> p a q", a=2)[:, :, lo:lo + P]
                    m = pool.do(lambda e, _, ev=ev: e.affine_select(out=ev, in_=ev, compare_op=ALU.is_ge, fill=0.0, base=0,
                                                                    pattern=[[0, 2], [1, P]], channel_multiplier=-1), s["masked"], apart=True)
                ready.append(m)
            last = (j - c * T + 1) * P >= (half + 1) * HALF

            def av():
                pe.wait(*ready)
                if j == 0 and half == 0:
                    pe.wait_latest(bank[4])
                for g in range(4):
                    e_at = slice(HALF * (g % 2) + lo, HALF * (g % 2 + 1))
                    m2 = pe.do(lambda e, _, g=g, e_at=e_at: e.matmul(PS[32 * g:32 * g + VW, 4, q], Va[:, j, g, :], HE[:, slots[g // 2], e_at],
                                                                     start=(j == 0 and half == 0), stop=last, skip_group_check=True), s["av"])
                for k in slots:
                    he_slot[k].marks = [m2]
                return m2, 4
            return av

        def context_in(c, grp, done):
            m, cb = done
            r = grp % 2
            act.wait(m)
            act.wait_latest(craw_slot[r])
            m = act.do(lambda e, _: e.activation(craw[:, r, :], psum(cb), ACT.Copy), s["craw_in"])
            bank[cb].marks = [m]
            return m

        def context_out(c, grp, m):
            r = grp % 2
            tb = 2 + r
            pe.wait(m)
            pe.wait_latest(bank[tb])
            for t in range(T):
                m = pe.do(lambda e, _, t=t: e.transpose(psum(tb, lo=t * P, hi=(t + 1) * P), craw[:, r, t * P:(t + 1) * P], ident[:, :]), s["ctx_t"])
            craw_slot[r].marks = [m]
            raw_t = psum(tb).rearrange("p (t g e) -> p t g e", t=T, g=4)
            dve.wait(m)
            if grp == 1:
                dve.wait_latest(prod_slot[0])
                dve.wait_latest(prod_slot[1])
            dve.wait(dve.do(lambda e, _: e.reciprocal(cinv[:, r, :, :], raw_t[:, :, :, HD]), s["ctx_rec"]))
            m = dve.do(lambda e, _: e.tensor_tensor(
                ctok[:, :, grp * 64:(grp + 1) * 64].rearrange("p t (g d) -> p t g d", g=4), raw_t[:, :, :, 0:HD],
                cinv[:, r, :, :].unsqueeze(3).to_broadcast([P, T, 4, HD]), ALU.mult), s["ctx_tok"])
            bank[tb].marks = [m]
            return m

        def context_parts(c, ready):
            pe.wait(ready)
            marks = []
            for k in range(DB):
                i = 2 + k
                pe.wait_latest(bank[i])
                for t in range(T):
                    m = pe.do(lambda e, _, t=t, k=k, i=i: e.transpose(psum(i, lo=t * P, hi=(t + 1) * P), ctok[:, t, k * P:(k + 1) * P], ident[:, :]), s["ctx_f"])
                act.wait(m)
                act.wait_latest(phl_slot[k])
                mh = act.do(lambda e, _, k=k, i=i: e.activation(PH[:, k, :], psum(i), ACT.Copy), s["ctx_hi"])
                dve.wait(mh)
                ml = dve.do(lambda e, _, k=k, i=i: e.tensor_tensor(PL[:, k, :], psum(i), PH[:, k, :].bitcast(F32), ALU.subtract), s["ctx_lo"])
                bank[i].marks = [ml]
                marks += [mh, ml]
            prod_slot[0].marks = prod_slot[1].marks = [m]
            return marks

        def finish(c, marks):
            pe.wait(*marks)
            X = xt[c]
            for u in range(T // 2):
                for t in (2 * u, 2 * u + 1):
                    for k in range(DB):
                        for a, b in ((PH, OH), (PH, OL), (PL, OH)):
                            m = pe.do(lambda e, _, t=t, k=k, a=a, b=b: e.matmul(
                                out_ps(t), a[:, k, t * P:(t + 1) * P], b[:, k, :], start=False,
                                stop=(k == DB - 1 and a is PL), skip_group_check=True), s["out_ps"])
                dve.wait(m)
                my = dve.do(lambda e, _, u=u: e.tensor_tensor(X[:, 2 * u:2 * u + 2, :], psum(u).rearrange("p (a d) -> p a d", a=2),
                                                              X[:, 2 * u:2 * u + 2, :], ALU.add), s["y"])
                bank[u].marks = [my]
            for h in range(2):
                phl_slot[h].marks = [m]
            sp.wait(my)
            mo = sp.do(lambda e, n: e.dma_start(outr[n, c], X[:, :, :]), s[f"stored{c}"], 16, apart=True)
            now[f"xt{c}"].marks = [mo]

        for c in range(NC):
            nxt = (c + 1) % NC
            load_x(nxt, (lambda n: n) if nxt else (lambda n: (n + 1) % NB))
            units = [(peaks_local, t, p) for t in range(T) for p in range(NL // 2)] + [(peaks_global, t, g) for t in range(T) for g in range(NG)]
            gone = [0]

            def peaks_upto(share):
                upto = int(len(units) * share)
                for f, t, a in units[gone[0]:upto]:
                    gone.append(f(c, t, a))
                gone[0] = upto

            hs = router_hidden(c)
            expert_x(c, 0)
            ml = router_logits(c, hs)
            peaks_upto(0.10)
            mw = router_weights(c, ml)
            peaks_upto(0.25)
            rows_in = router_rows(c, mw)
            expert_c(c, 0, rows_in)
            open_out(c, rows_in)
            for j in range(1, 8):
                expert_x(c, j)
                peaks_upto(0.25 + 0.125 * j if j < 6 else 1.0)
                if j == 6:
                    peak_in = peaks_to_rows(c, gone[-1])
                if j == 5:
                    normalised = normalise(nxt)
                expert_c(c, j, rows_in)
                mix(c, j - 1)
            turn_tokens(nxt, normalised)
            parts_block(1, 0)
            mix(c, 7)
            between = [lambda: parts_block(1, 1), lambda: parts_block(0, 0), lambda: parts_block(0, 1)]
            late, contexts = [], []

            def flush(keep):
                while len(late) > keep:
                    grp, av, closes = late.pop(0)
                    done = av()
                    if closes:
                        contexts.append((grp, context_in(c, grp, done)))
                        if len(contexts) > 1:
                            g_, m_ = contexts.pop(0)
                            contexts_out.append(context_out(c, g_, m_))

            contexts_out = []
            for grp in range(1, 1 + NL // 4):
                for half in range(2):
                    late.append((grp, attend_local(c, grp, half, peak_in), half == 1))
                    flush(1)
                    if half == 0:
                        between.pop(0)()
            tiles = [(j, half) for j in range((c + 1) * T) for half in range(2) if (half + 1) * (C // 2) > (j - c * T) * P]
            for j, half in tiles:
                late.append((0, attend_global(c, j, half, peak_in), (j, half) == tiles[-1]))
                flush(1)
            now["q"].marks = [Mark(s["st"], s["st"].n)]
            now["kl"].marks = now["kg"].marks = now["q"].marks
            keep_keys(nxt)
            load_stacks(nxt)
            flush(0)
            now["va"].marks = [Mark(s["av"], s["av"].n)] + now["v_shift"].marks if c else [Mark(s["av"], s["av"].n)]
            now["vs"].marks = [Mark(s["av"], s["av"].n)]
            values(nxt)
            for g_, m_ in contexts:
                contexts_out.append(context_out(c, g_, m_))
            finish(c, context_parts(c, contexts_out[-1]))

        with nc.Block() as block:
            @block.sync
            def _(e):
                for t_ in s.values():
                    if t_.n:
                        e.sem_inc(t_.sem, t_.n)

        body = (pe, act, dve, pool, sp)

        def looped(queue):
            def program(e):
                with e.Fori(0, NB) as n:
                    queue.write(e, n, waits_apart=queue is sp)
                if queue is sp:
                    for name in ("stored0", "stored1", "kq_in", "vs_in"):
                        e.wait_ge(s[name].sem, s[name].n * (NB + 1))
            return program

        with nc.Block() as block:
            block.tensor(looped(body[0]))
            block.scalar(looped(body[1]))
            block.vector(looped(body[2]))
            block.gpsimd(looped(body[3]))
            block.sync(looped(body[4]))


_INS = ['L0_attn_x', 'L0_attn_w_qkv', 'L0_attn_b_qkv', 'L0_attn_w_out', 'L0_attn_b_out', 'L0_ffn_W_Q', 'L0_ffn_W_K',
        'L0_ffn_W_O', 'L0_ffn_W_inv', 'L0_ffn_V_fwd', 'L0_ffn_W_fwd', 'L0_ffn_U_fwd', 'L0_ffn_b_fwd', 'L0_ffn_V_inv',
        'L0_ffn_W_inv_exp', 'L0_ffn_U_inv', 'L0_ffn_b_inv', 'L0_ffn_router_w1', 'L0_ffn_router_b1', 'L0_ffn_router_w2',
        'L0_ffn_router_b2', 'L0_ffn_alpha_bi', 'L0_ffn_expert_bias']


def kernel(**inputs):
    import numpy as _np
    import concourse.bacc as _bacc
    from concourse import mybir as _mybir
    from concourse.bass_utils import run_bass_kernel_spmd as _run

    nc = _bacc.Bacc("TRN2", target_bir_lowering=False, num_devices=1)
    arrays, args = {}, []
    for name in _INS:
        a = _np.ascontiguousarray(inputs[name])
        if a.ndim == 0:
            a = a.reshape(1)
        arrays[f"in_{name}_dram"] = a
        args.append(nc.dram_tensor(f"in_{name}_dram", a.shape, _mybir.dt.from_np(a.dtype), kind="ExternalInput").ap())
    shape = tuple(inputs['L0_attn_x'].shape)
    args.append(nc.dram_tensor("out_0_dram", shape, _mybir.dt.float32, kind="ExternalOutput").ap())
    with nc.allow_non_contiguous_dma("small weights are read by columns once"):
        mixer_layer(nc, *args)
    r = _run(nc, [arrays], core_ids=[0])
    return r.results[0]["out_0_dram"]
```

```python
from contextlib import ExitStack

from concourse import mybir

F32 = mybir.dt.float32
F32R = mybir.dt.float32r
BF16 = mybir.dt.bfloat16
I32 = mybir.dt.int32
ALU = mybir.AluOpType
ACT = mybir.ActivationFunctionType
AX_X = mybir.AxisListType.X

P = 128
WINDOW = 64
N_GLOBAL = 4
LN_EPS = 1e-5
MASKED = -1e30
LOWEST = -3e38
RSQRT_START = 0x5F3759DF

EARLY_LOCAL = 10
FIRST_LOCAL = 3
LAST_LOCALS = 2
FILLS = 47


class Tally:

    def __init__(self, sem):
        self.sem = sem
        self.n = 0


class Mark:

    def __init__(self, tally, value):
        self.tally, self.value = tally, value


class Latest:

    def __init__(self, name):
        self.name, self.marks = name, []


class Queue:

    def __init__(self):
        self.items = []

    def wait(self, *marks):
        for m in marks:
            self.items.append(("wait", m))

    def wait_latest(self, thing):
        if thing.marks:
            self.wait(*thing.marks)
        else:
            self.items.append(("wait_last_turn", thing))

    def do(self, fn, tally=None, by=1, apart=False):
        if apart:
            self.items.append(("do", lambda e, _: e.nop(nofuse=True), None, 0))
        if tally is None:
            self.items.append(("do", fn, None, 0))
            return None
        tally.n += by
        self.items.append(("do", fn, tally, by))
        return Mark(tally, tally.n)

    def write(self, eng, turn=None, waits_apart=False):
        seen, due = {}, {}
        for item in self.items:
            if item[0] == "wait":
                due[item[1].tally] = max(item[1].value, due.get(item[1].tally, -(1 << 30)))
            elif item[0] == "wait_last_turn":
                for m in item[1].marks if turn is not None else ():
                    due[m.tally] = max(m.value - m.tally.n, due.get(m.tally, -(1 << 30)))
            else:
                for tally, value in due.items():
                    if seen.get(tally, -(1 << 30)) < value:
                        seen[tally] = value
                        eng.wait_ge(tally.sem, value if turn is None else turn * tally.n + (tally.n + value))
                        if waits_apart:
                            eng.nop(nofuse=True)
                due = {}
                _, fn, tally, by = item
                ins = fn(eng, turn)
                if tally is not None:
                    ins.then_inc(tally.sem, by)
        for tally, value in due.items():
            eng.wait_ge(tally.sem, value if turn is None else turn * tally.n + (tally.n + value))


def mixer_layer(
    nc, x, w_qkv, b_qkv, w_out, b_out, W_Q, W_K, W_O, W_inv, V_fwd, W_fwd, U_fwd, b_fwd,
    V_inv, W_inv_exp, U_inv, b_inv, router_w1, router_b1, router_w2, router_b2, alpha, expert_bias, out,
):
    NB, S, D = x.shape
    KE, _, R = V_fwd.shape
    HD = 16
    NH = D // HD
    NG = N_GLOBAL
    NL = NH - NG
    KR = KE * R
    DB = D // P
    KB = KR // P
    C = 512
    NC = S // C
    T = C // P
    ST = S // P
    SCALE = float(HD) ** -0.5
    assert DB == 2 and NC == 2 and KR == 512 and NG == 4 and NL % 4 == 0 and C // WINDOW == 8
    COL_Q, COL_K, COL_V = 0, D, 2 * D
    COL_R = 3 * D
    COL_X = COL_R + 2 * D
    COL_C = COL_X + 2 * KR
    NCOL = COL_C + 2 * KR
    G16 = 6 * HD
    KSTK = G16 + 3
    RIGHT = (0, 1, 2, 0, 1, 0)
    STACK = ((slice(0, 3 * HD), None), (slice(3 * HD, 4 * HD), (0, 1)), (slice(4 * HD, 5 * HD), (1, 2)), (slice(5 * HD, 6 * HD), (0, 2)))
    VW = HD + 1

    ctx = ExitStack()
    with ctx:
        def sb(name, shape, dt=F32):
            return ctx.enter_context(nc.sbuf_tensor(name, shape, dt))

        def tally(name):
            return Tally(ctx.enter_context(nc.semaphore(name)))

        WH = sb("WH", [P, DB, NCOL], F32R)
        WL = sb("WL", [P, DB, NCOL], F32R)
        UH = sb("UH", [P, 2 * KB, D], F32R)
        UL = sb("UL", [P, 2 * KB, D], F32R)
        OH = sb("OH", [P, DB, D], F32R)
        OL = sb("OL", [P, DB, D], F32R)
        bias_rows = sb("bias_rows", [KSTK, D], BF16)
        spread = sb("spread", [KSTK, 2 * KB, P], BF16)
        W2 = sb("W2", [P, DB, KE])
        ident = sb("ident", [P, P])
        ident_b = sb("ident_b", [P, P], BF16)
        band = sb("band", [P, 2, P + WINDOW])
        strip = sb("strip", [P, C])
        mask_l = sb("mask_l", [P, WINDOW], BF16)
        mask_g = sb("mask_g", [P, P], BF16)
        q_bias = sb("q_bias", [P, DB])
        k_bias = sb("k_bias", [P, DB])
        r_bias = sb("r_bias", [P, DB])
        l_bias = sb("l_bias", [P, 2])
        inv_n = sb("inv_n", [P, ST])

        QS_W = NH * C // 2
        KL_W = NL * (C + WINDOW) // 2
        KG_W = NG * S // 2
        PT_W = 2 * 3 * DB * C // 2
        AREA = QS_W + KL_W + KG_W + PT_W
        area = sb("area", [P, AREA])
        at = [0]

        def carve(width):
            a = area[:, at[0]:at[0] + width]
            at[0] += width
            return a

        QS = carve(QS_W).bitcast(BF16).rearrange("p (h t) -> p h t", h=NH)
        KL = carve(KL_W).bitcast(BF16).rearrange("p (h t) -> p h t", h=NL)
        KG = carve(KG_W).bitcast(BF16).rearrange("p (h t) -> p h t", h=NG)
        parts = carve(PT_W).bitcast(BF16).rearrange("p (w i b t) -> p w i b t", w=2, i=3, b=DB)

        xt = [sb(f"xt{i}", [P, T, D]) for i in range(2)]
        tok = sb("tok", [P, T, D])
        XH = sb("XH", [P, DB, C], F32R)
        XL = sb("XL", [P, DB, C], F32R)
        CH = sb("CH", [P, DB, C], F32R)
        CL = sb("CL", [P, DB, C], F32R)
        rest = sb("rest", [P, 2, C])
        carry = sb("carry", [P, DB])
        stats = sb("stats", [P, T, 6])
        mv = sb("mv", [P, T, 2])
        var = sb("var", [P, 4, T])
        unused = sb("unused", [P, 1])
        alphac = sb("alpha_column", [P, 1])[:, :]
        Va = sb("Va", [P, ST, NH, VW])
        Vs = sb("Vs", [P, T, NL, VW])
        HE = sb("HE", [P, 4, C])
        gate = sb("gate", [P, 4, T, 2 * KE])
        gsum = sb("gsum", [P, 4, T * 2])
        wstack = sb("wstack", [P, T, KSTK], BF16)
        WT = sb("WT", [KSTK, C], BF16)
        prod = sb("prod", [P, 3, C])
        PH = sb("PH", [P, 2, C], F32R)
        PL = sb("PL", [P, 2, C], F32R)
        positions = sb("positions", [P, ST], I32)
        peak = sb("peak", [P, T, NH])
        peak_rest = sb("peak_rest", [P, T, NH])
        peak_part = sb("peak_part", [P, T, NG])
        peak_t = [sb(f"peak_t_{n}", [P, T, 3 * k], BF16) for n, k in (("local", NL), ("global", NG))]
        peak_f = sb("peak_f", [3 * NL, C], BF16)
        craw = sb("craw", [P, 2, C])
        ctok = sb("ctok", [P, T, D])
        cinv = sb("cinv", [P, 2, T, 4])
        logit_f = craw[:, 0, :]
        PS = ctx.enter_context(nc.psum_tensor("PS", [P, 8, 512], F32))

        parts_d = nc.dram_tensor("parts_d", (2, D, 3, C), BF16, kind="Internal").ap()
        peak_d = [nc.dram_tensor(f"peak_d_{n}", (3 * k, C), BF16, kind="Internal").ap() for n, k in (("local", NL), ("global", NG))]
        xr = x.rearrange("n (c t p) d -> n c p t d", c=NC, t=T)
        outr = out.rearrange("n (c t p) d -> n c p t d", c=NC, t=T)

        names = ("x_in0 x_in1 stat xn turned xhi xlo summed chi clo proj_kq part1 part_dve parts_out0 parts_out1 local_in global_in "
                 "projv v_in vs_in vs_zero keys_kept proj_r hidden logits logit_b gate_t gate_max gate_exp gates wt_t wt_in "
                 "xv_ps w_ps cum_ps xv_in xvw xvwc phi plo mixed scores peaks peak_parts peak_turned peak_copied "
                 "peak_out0 peak_out1 peak_in0 peak_in1 st exped av craw_in ctx_t ctx_rec ctx_tok ctx_f ctx_hi ctx_lo out_ps y stored0 stored1")
        front_names = ("x_in0 stat xn turned xhi xlo summed chi clo proj_kq part1 part_dve parts_out0 parts_out1 local_in global_in projv v_in "
                       "vs_in vs_zero keys_kept proj_r hidden logits logit_b scores peaks")
        things = ("tok tok_free x_free x c_free c carry parts0 parts1 parts_d0 parts_d1 local global va vs stats logits gate wstack wt rows peak0 peak1 "
                  "peak_t0 peak_t1 peak_f peak_d0 peak_d1 ctok kept local_in global_in v v_shift xt0_in xt1_in xt0 xt1")
        pe, act, dve, pool, sp = (Queue() for _ in range(5))
        s = {n: tally("first_" + n) for n in front_names.split()}
        bank = [Latest(f"bank {i}") for i in range(8)]
        now = {n: Latest(n) for n in things.split()}
        rest_slot = [Latest(f"rest {i}") for i in range(2)]
        he_slot = [Latest(f"hidden/exp {i}") for i in range(4)]
        prod_slot = [Latest(f"product {i}") for i in range(3)]
        phl_slot = [Latest(f"split product {i}") for i in range(2)]
        craw_slot = [Latest(f"raw context {i}") for i in range(2)]

        def psum(i, rows=P, lo=0, hi=512):
            return PS[0:rows, i, lo:hi]

        def summed_mms(ps, pairs, tl, midway=None):
            n = len(pairs)
            for k, (a, b) in enumerate(pairs):
                if midway and k == n // 2:
                    midway()
                m = pe.do(lambda e, _, a=a, b=b, k=k: e.matmul(ps, a, b, start=(k == 0), stop=(k == n - 1), skip_group_check=True),
                          tl if k == n - 1 else None)
            return m

        def project(i, col, src_h, src_l, tl, midway=None):
            pairs = []
            for k in range(DB):
                wh, wl = WH[:, k, col:col + P], WL[:, k, col:col + P]
                pairs += [(wh, src_h[:, k, :]), (wh, src_l[:, k, :]), (wl, src_h[:, k, :])]
            pe.wait_latest(bank[i])
            return summed_mms(psum(i), pairs, tl, midway)

        def load_x(c, of):
            sp.wait_latest(now[f"xt{c}"])
            now[f"xt{c}_in"].marks = [sp.do(lambda e, n: e.dma_start(xt[c][:, :, :], xr[of(n), c]), s[f"x_in{c}"], 16, apart=True)]

        def normalise(c):
            X = xt[c]
            v, a1, a2, y = (var[:, k, :] for k in range(4))

            def moments():
                dve.wait_latest(now[f"xt{c}_in"])
                dve.wait_latest(now["stats"])
                for t in range(T):
                    m = dve.do(lambda e, _, t=t: e.bn_stats(stats[:, t, :], X[:, t, :]), s["stat"])
                dve.wait(m)
                for t in range(T):
                    m = dve.do(lambda e, _, t=t: e.bn_aggr(mv[:, t, :], stats[:, t, :]), s["stat"], apart=(t == 0))
                dve.wait(m)
                dve.wait(dve.do(lambda e, _: e.tensor_scalar(v, mv[:, :, 1], LN_EPS, None, ALU.add), s["stat"]))

            def start():
                dve.wait(dve.do(lambda e, _: e.tensor_scalar(a1.bitcast(I32), v.bitcast(I32), 1, None, ALU.logical_shift_right), s["stat"]))
                dve.wait(dve.do(lambda e, _: e.tensor_scalar(y.bitcast(I32), a1.bitcast(I32), -1, RSQRT_START, ALU.mult, ALU.add), s["stat"]))

            def square():
                dve.wait(dve.do(lambda e, _: e.tensor_tensor(a2, y, y, ALU.mult), s["stat"]))
                dve.wait(dve.do(lambda e, _: e.tensor_tensor(a1, a2, v, ALU.mult), s["stat"]))

            def correct():
                dve.wait(dve.do(lambda e, _: e.tensor_scalar(a2, a1, -0.5, 1.5, ALU.mult, ALU.add), s["stat"]))
                dve.wait(dve.do(lambda e, _: e.tensor_tensor(y, a2, y, ALU.mult), s["stat"]))

            def scale():
                dve.wait_latest(now["tok_free"])
                for t in range(T):
                    m = dve.do(lambda e, _, t=t: e.tensor_scalar(tok[:, t, :], X[:, t, :], mv[:, t, 0:1], var[:, 3, t:t + 1],
                                                                 ALU.subtract, ALU.mult), s["xn"])
                now["stats"].marks = now["tok"].marks = [m]

            return [moments, start] + 3 * [square, correct] + [scale]

        def turn_tokens(c):
            pe.wait_latest(now["tok"])
            his, los, chis, clos = [], [], [], []
            for k in range(DB):
                i = 2 + k
                pe.wait_latest(bank[i])
                for t in range(T):
                    mt = pe.do(lambda e, _, t=t, k=k, i=i: e.transpose(psum(i, lo=t * P, hi=(t + 1) * P), tok[:, t, k * P:(k + 1) * P], ident[:, :]), s["turned"])
                act.wait(mt)
                if k == 0:
                    act.wait_latest(now["x_free"])
                his.append(act.do(lambda e, _, k=k, i=i: e.activation(XH[:, k, :], psum(i), ACT.Copy), s["xhi"]))
                dve.wait(his[-1])
                los.append(dve.do(lambda e, _, k=k, i=i: e.tensor_tensor(XL[:, k, :], psum(i), XH[:, k, :].bitcast(F32), ALU.subtract), s["xlo"]))
                dve.wait_latest(rest_slot[k])
                if c:
                    dve.wait_latest(now["carry"])
                init = carry[:, k:k + 1] if c else 0.0
                ms = dve.do(lambda e, _, k=k, i=i, init=init: e.tensor_tensor_scan(
                    rest[:, k, :], psum(i), XH[:, k, :].bitcast(F32), init, ALU.add, ALU.bypass), s["summed"])
                bank[i].marks = [ms]
                act.wait(ms)
                if k == 0:
                    act.wait_latest(now["c_free"])
                mch = act.do(lambda e, _, k=k: e.activation(CH[:, k, :], rest[:, k, :], ACT.Copy), s["chi"])
                pool.wait(mch)
                mcl = pool.do(lambda e, _, k=k: e.tensor_tensor(CL[:, k, :], rest[:, k, :], CH[:, k, :].bitcast(F32), ALU.subtract), s["clo"])
                rest_slot[k].marks = [mcl]
                if c == 0:
                    dve.wait(ms)
                    mc = dve.do(lambda e, _, k=k: e.tensor_copy(carry[:, k:k + 1], rest[:, k, C - 1:C]), s["summed"])
                    now["carry"].marks = [mc]
                    rest_slot[k].marks.append(mc)
            now["tok_free"].marks = [mt]
            now["x"].marks = [his[-1], los[-1]]
            now["c"].marks = [mch, mcl]

        def parts_block(w, b):
            col, bias = ((COL_K, k_bias) if w else (COL_Q, q_bias))
            i = r = b
            i += 2
            if b == 0:
                act.wait_latest(now[f"parts{w}"])
                dve.wait_latest(now[f"parts{w}"])
            pe.wait_latest(now["x"])
            m = project(i, col + b * P, XH, XL, s["proj_kq"])
            p1, p2, p3 = (parts[:, w, j if w else 2 - j, b, :] for j in range(3))
            left = rest[:, r, :]
            act.wait(m)
            m1 = act.do(lambda e, _: e.activation(p1, psum(i), ACT.Identity, bias=bias[:, b:b + 1]), s["part1"])
            dve.wait(m1)
            dve.wait_latest(rest_slot[r])
            m2 = dve.do(lambda e, _: e.scalar_tensor_tensor(out=left, in0=psum(i), scalar=bias[:, b:b + 1], in1=p1,
                                                            op0=ALU.add, op1=ALU.subtract), s["part_dve"])
            bank[i].marks = [m2]
            dve.wait(m2)
            m3 = dve.do(lambda e, _: e.tensor_copy(p2, left), s["part_dve"])
            dve.wait(m3)
            m4 = dve.do(lambda e, _: e.tensor_tensor(p3, left, p2, ALU.subtract), s["part_dve"])
            rest_slot[r].marks = [m4]
            if b == DB - 1:
                sp.wait(m1, m4)
                sp.wait_latest(now[f"parts_d{w}"])
                mo = sp.do(lambda e, _: e.dma_start(parts_d[w].rearrange("(b p) i t -> p i b t", p=P), parts[:, w, :, :, :]), s[f"parts_out{w}"], 16)
                now[f"parts{w}"].marks = [mo]

        def keep_keys(c):
            dve.wait_latest(now["local"])
            if c == 0:
                mk = dve.do(lambda e, _: e.memset(KL[0:KSTK, :, 0:WINDOW], 0.0), s["keys_kept"])
            else:
                mk = dve.do(lambda e, _: e.tensor_copy(KL[0:KSTK, :, 0:WINDOW], KL[0:KSTK, :, C:C + WINDOW]), s["keys_kept"])
            now["kept"].marks = [mk]

        def load_stacks(c, kind):
            sp.wait_latest(now["kept" if kind == "local" else "global"])
            for w in (1, 0):
                sp.wait_latest(now[f"parts{w}"])
                by_head = parts_d[w].rearrange("(h d) i t -> d i h t", d=HD)
                for rows, i in STACK:
                    if i is None:
                        src = parts_d[w].rearrange("(h d) i t -> (d i) h t", d=HD)
                    else:
                        src = by_head[:, i[1 - w], :, :]
                    if kind == "local":
                        dst, src = (KL[rows, :, WINDOW:] if w else QS[rows, NG:, :]), src[:, NG:, :]
                    else:
                        dst, src = (KG[rows, :, c * C:(c + 1) * C] if w else QS[rows, 0:NG, :]), src[:, 0:NG, :]
                    mi = sp.do(lambda e, _, dst=dst, src=src: e.dma_start(dst, src), s[kind + "_in"], 16)
            now[kind + "_in"].marks = [mi]
            for w in range(2):
                now[f"parts_d{w}"].marks = [mi] if kind == "local" else now[f"parts_d{w}"].marks + [mi]

        def values(c):
            pe.wait_latest(now["x"])
            act.wait_latest(now["va"])
            for u in range(T // 2):
                i = 2 + u
                pe.wait_latest(bank[i])
                for a in range(2):
                    t = 2 * u + a
                    pairs = []
                    for k in range(DB):
                        wh, wl = WH[:, k, COL_V:COL_V + D], WL[:, k, COL_V:COL_V + D]
                        xh, xl = XH[:, k, t * P:(t + 1) * P], XL[:, k, t * P:(t + 1) * P]
                        pairs += [(xh, wh), (xh, wl), (xl, wh)]
                    m = summed_mms(psum(i, lo=a * D, hi=(a + 1) * D), pairs, s["projv"])
                act.wait(m)
                tt = c * T + 2 * u
                mv_ = act.do(lambda e, _, i=i, tt=tt: e.activation(
                    Va[:, tt:tt + 2, :, 0:HD], psum(i).rearrange("p (a h d) -> p a h d", a=2, h=NH), ACT.Copy), s["v_in"])
                bank[i].marks = [mv_]
            now["v"].marks = [mv_]
            sp.wait(mv_)
            sp.wait_latest(now["vs"])
            t0 = c * T
            now["v_shift"].marks = []
            if c == 0:
                pool.wait_latest(now["vs"])
                now["v_shift"].marks = [pool.do(lambda e, _: e.memset(Vs[0:WINDOW, 0, :, :], 0.0), s["vs_zero"], apart=True)]
                sp.do(lambda e, _: e.dma_start(Vs[0:WINDOW, 1:T, :, :], Va[WINDOW:P, 0:T - 1, NG:, :]), s["vs_in"], 16)
            else:
                sp.do(lambda e, _: e.dma_start(Vs[0:WINDOW, :, :, :], Va[WINDOW:P, t0 - 1:t0 + T - 1, NG:, :]), s["vs_in"], 16)
            now["v_shift"].marks.append(sp.do(lambda e, _: e.dma_start(Vs[WINDOW:P, :, :, :], Va[0:WINDOW, t0:t0 + T, NG:, :]), s["vs_in"], 16))

        def router_hidden(c, j):
            i = (4, 7)[j % 2]
            pe.wait_latest(now["x"])
            m = project(i, COL_R + j * P, XH, XL, s["proj_r"])
            act.wait(m)
            act.wait_latest(he_slot[j])
            m = act.do(lambda e, _: e.activation(HE[:, j, :], psum(i), ACT.Gelu, bias=r_bias[:, j % DB:j % DB + 1]), s["hidden"])
            bank[i].marks = [m]
            return m

        def router_logits(c, hidden):
            pe.wait(hidden)
            pe.wait_latest(bank[7])
            for j in range(2 * DB):
                m = pe.do(lambda e, _, j=j: e.matmul(PS[32 * j:32 * j + KE, 7, :], W2[:, j % DB, :], HE[:, j, :], start=True, stop=True,
                                                     skip_group_check=True), s["logits"])
                he_slot[j].marks = [m]
            act.do(lambda e, _: e.activation(unused[:, :], l_bias[:, 0:1], ACT.Exp, scale=0.0))
            act.wait(m)
            act.wait_latest(craw_slot[0])
            ml = act.do(lambda e, _: e.activation(logit_f, psum(7), ACT.Identity, bias=l_bias[:, 0:1]), s["logit_b"])
            bank[7].marks = [ml]
            now["logits"].marks = [ml]

        turns = {"score": 0, "exp": 0}
        local_pairs = [(t, pair) for t in range(T) for pair in range(NL // 2)]
        early_pairs, later_pairs = local_pairs[:EARLY_LOCAL], local_pairs[EARLY_LOCAL:]

        def score_bank():
            turns["score"] ^= 1
            return 5 + turns["score"]

        def peaks_local(c, t, pair):
            i = score_bank()
            if t == 0 and pair == 0:
                pe.wait_latest(now["local_in"])
                pe.wait_latest(now["kept"])
                dve.wait_latest(now["peak0"])
            pe.wait_latest(bank[i])
            for a in range(2):
                l = 2 * pair + a
                m = pe.do(lambda e, _, a=a, l=l: e.matmul(psum(i, lo=256 * a, hi=256 * a + BW), QS[0:G16, NG + l, t * P:(t + 1) * P],
                                                          KL[0:G16, l, t * P:t * P + BW], start=(a == 0), stop=(a == 1),
                                                          skip_group_check=True), s["scores"])
            dve.wait(m)
            which = 1 if c == 0 and t == 0 else 0
            for a in range(2):
                h = NG + 2 * pair + a
                ps = psum(i, lo=256 * a, hi=256 * a + BW)
                m = dve.do(lambda e, _, ps=ps, h=h: e.tensor_tensor_reduce(
                    ps, ps, band[:, which, :], 1.0, LOWEST, ALU.add, ALU.max, peak[:, t, h:h + 1]), s["peaks"], apart=(a == 0))
            bank[i].marks = [m]
            return m

        s_raw = [tally(f"raw_loaded{i}") for i in range(5)]
        s_pe0 = tally("setup_pe")
        s_act0 = tally("setup_act")
        s_dve0 = tally("setup_dve")
        s_pool0 = tally("setup_pool")
        s_put0 = tally("setup_rows_put")
        at[0] = 0

        def raw(shape):
            n = shape[0] * shape[1]
            return carve(n).rearrange("p (a b) -> p a b", a=shape[0])

        rWQ, rWK, rWI, rWO, rR1, tWI, tR1, rOUT = (raw((DB, D)) for _ in range(8))
        rQKV = prod[:, :, :].rearrange("p a b -> p (a b)").rearrange("p (b d) -> p b d", b=DB)
        tWO = craw[:, 1, :].rearrange("p (b d) -> p b d", b=DB)
        gQ, gK = rWI, rR1
        rV = [raw((DB, KR)) for _ in range(4)]
        rU = [t_[:, :, :].rearrange("p t d -> p (t d)").rearrange("p (b k) -> p b k", b=DB) for t_ in (xt[1], ctok)]
        assert at[0] <= AREA - PT_W
        rows8 = HE[0:KE, 0, :]
        rows8b = HE[0:KE, 1, :]
        columns = HE[:, 2, 0:64]
        borow = HE[0:1, 2, 256:256 + D]
        row0 = gate[0:1, :, :, :].rearrange("a b t k -> a (b t k)")
        alpha1 = HE[0:1, 3, 0:1]
        ones1 = HE[0:1, 3, 8:8 + P]
        brow = [prod[0:KE, 0, 0:D], prod[0:KE, 0, D:2 * D], row0]
        brest = [[prod[0:KE, 1 + j, 0:D], prod[0:KE, 1 + j, D:2 * D]] for j in range(2)] + [[craw[0:1, 0, 0:D], craw[0:1, 0, D:2 * D]]]
        bpart = [[rest[0:KE, j, D // 2 * i:D // 2 * (i + 1)].bitcast(BF16) for i in range(3)] for j in range(2)] + \
                [[WT[0:1, 0:D], WT[0:1, D:2 * D], peak_f[0:1, 0:D]]]

        def load(dst, src, group):
            return sp.do(lambda e, _: e.dma_start(dst, src), s_raw[group], 16)

        for view in (l_bias[:, :], rows8b[:, D:D + P]):
            blank = dve.do(lambda e, _, view=view: e.memset(view, 0.0), s_dve0)
        load_x(0, lambda n: 0)
        sp.wait(blank)
        load_q = load(rQKV, w_qkv.rearrange("(b p) d -> p b d", p=P), 4)
        load(rows8b[:, 0:D], b_inv, 0)
        load(rows8[:, 0:D], router_w2, 0)
        load(rows8[:, D:2 * D], b_fwd, 0)
        load(rows8b[0:6, D:D + P], b_qkv.rearrange("(a b) -> a b", b=P), 0)
        load(rows8b[6:8, D:D + P], router_b1.rearrange("(a b) -> a b", b=P), 0)
        load(borow, b_out.rearrange("(a d) -> a d", a=1), 0)
        load(alpha1, alpha.rearrange("(a d) -> a d", a=1), 0)
        for w in range(2):
            l_at = slice(64 * w, 64 * w + KE)
            load(l_bias[l_at, 0:1], router_b2.rearrange("(k a) -> k a", a=1), 0)
            load_0 = load(l_bias[l_at, 1:2], expert_bias.rearrange("(k a) -> k a", a=1), 0)
        for dst, src in ((rWI, W_inv), (rWQ, W_Q), (rWK, W_K), (rR1, router_w1), (rWO, W_O)):
            load_1 = load(dst, src.rearrange("(b p) d -> p b d", p=P), 1)
        for dst, src in zip(rV, (V_fwd, W_inv_exp, W_fwd, V_inv)):
            for b in range(DB):
                load_2 = load(dst[:, b, :].rearrange("p (k r) -> p k r", k=KE), src[:, b * P:(b + 1) * P, :].rearrange("k p r -> p k r"), 2)
        load(rOUT, w_out.rearrange("(b p) d -> p b d", p=P), 3)
        for dst, src in zip(rU, (U_fwd, U_inv)):
            for b in range(DB):
                load_3 = load(dst[:, b, :].rearrange("p (k r) -> p k r", k=KE), src[:, b * P:(b + 1) * P, :].rearrange("k p r -> p k r"), 3)

        for name in names.split():
            sp.do(lambda e, _, name=name: e.sem_inc(s[name].sem, s[name].n) if s[name].n else None)

        for view, value in ((ident[:, :], 0.0), (ident_b[:, :], 0.0), (band[:, :, :], 0.0), (strip[:, :], 0.0),
                            (spread[:, :, :], 0.0), (mask_l[:, :], 0.0), (mask_g[:, :], 0.0)):
            cleared = dve.do(lambda e, _, view=view, value=value: e.memset(view, value), s_dve0)
        pool.wait(cleared)

        def select(view, pattern, base, cm, op=ALU.is_ge, fill=MASKED):
            m = pool.do(lambda e, _: e.affine_select(out=view, in_=view, compare_op=op, fill=fill, base=base,
                                                     pattern=pattern, channel_multiplier=cm), s_pool0)
            pool.wait(m)
            return m

        for view in (ident[:, :], ident_b[:, :]):
            ident_in = select(view, [[1, P]], 0, -1, ALU.not_equal, 1.0)
        BW = P + WINDOW
        for v in range(2):
            select(band[:, v, :], [[1, BW]], 0, -1)
            select(band[:, v, :], [[-1, BW]], WINDOW, 1)
        select(band[:, 1, :], [[1, BW]], -WINDOW, 0)
        select(strip[:, :], [[-1, C]], C - P, 1)
        select(mask_l[:, :], [[-1, WINDOW]], 0, 1)
        select(mask_l[:, :], [[1, WINDOW]], WINDOW, -1)
        select(mask_g[:, :], [[1, P]], 0, -1)
        for first in (0, 3 * HD, 5 * HD):
            view = spread[:, :, :].rearrange("r j (a m) -> r (j a) m", a=2)
            select(view, [[-1, 4 * KB], [0, R]], -first, 1, ALU.not_equal, 1.0)
        count = positions[:, :]
        counted = pool.do(lambda e, _: e.iota(count, pattern=[[P, ST]], base=1, channel_multiplier=1), s_pool0)

        pe.wait(ident_in)
        for piece in normalise(0):
            piece()
        turn_tokens(0)

        for view, value in ((ones1, 1.0), (wstack[:, :, :], 1.0), (Va[:, :, :, :], 1.0)):
            cleared = dve.do(lambda e, _, view=view, value=value: e.memset(view, value), s_dve0)
        dve.wait(counted)
        dve.wait(dve.do(lambda e, _: e.tensor_copy(inv_n[:, :], count), s_dve0))
        dve.wait(dve.do(lambda e, _: e.reciprocal(inv_n[:, :], inv_n[:, :]), s_dve0))
        for i in (4, 7):
            cleared = dve.do(lambda e, _, i=i: e.memset(PS[:, i, :], 0.0), s_dve0)
            bank[i].marks = [cleared]
        dve.wait(load_0)
        for w in range(2):
            l_at = slice(64 * w, 64 * w + KE)
            dve.do(lambda e, _, l_at=l_at: e.tensor_tensor(l_bias[l_at, 0:1], l_bias[l_at, 0:1], l_bias[l_at, 1:2], ALU.add), s_dve0)
        bank_of = [0]

        def next_bank():
            i = bank_of[0] % 8
            bank_of[0] += 1
            pe.wait_latest(bank[i])
            return i

        def product(rows, lhsTs, rhss, n):
            i = next_bank()
            for k, (a, b) in enumerate(zip(lhsTs, rhss)):
                m = pe.do(lambda e, _, a=a, b=b, k=k: e.matmul(PS[0:rows, i, 0:n], a, b, start=(k == 0), stop=(k == len(lhsTs) - 1)), s_pe0)
            return i, m

        def put_split(hi, lo, src, ready, scale=None):
            act.wait(ready)
            if scale is None:
                h = act.do(lambda e, _: e.activation(hi, src, ACT.Copy), s_act0)
                dve.wait(h)
                return dve.do(lambda e, _: e.tensor_tensor(lo, src, hi.bitcast(F32), ALU.subtract), s_dve0)
            h = act.do(lambda e, _: e.activation(hi, src, ACT.Identity, scale=scale), s_act0)
            dve.wait(h)
            return dve.do(lambda e, _: e.scalar_tensor_tensor(out=lo, in0=src, scalar=scale, in1=hi.bitcast(F32),
                                                              op0=ALU.mult, op1=ALU.subtract), s_dve0)

        pe.wait(load_0)
        act.wait(load_0)
        i = next_bank()
        for k, src in enumerate([rows8[:, b * P:(b + 1) * P] for b in range(4)] + [rows8b[:, b * P:(b + 1) * P] for b in range(3)]):
            m = pe.do(lambda e, _, k=k, src=src, i=i: e.transpose(PS[:, i, k * KE:(k + 1) * KE], src, ident[0:KE, 0:KE]), s_pe0)
        act.wait(m)
        m = act.do(lambda e, _, i=i: e.activation(columns[:, 0:7 * KE], PS[:, i, 0:7 * KE], ACT.Copy), s_act0)
        bank[i].marks = [m]
        act.wait(m)
        pe.wait(m)
        column = lambda k: columns[:, k * KE:(k + 1) * KE]
        act.do(lambda e, _: e.activation(W2[:, :, :].rearrange("p b k -> p (b k)"), columns[:, 0:2 * KE], ACT.Copy), s_act0)
        for dst, k in ((q_bias, 0), (k_bias, 2), (r_bias, 6)):
            m = act.do(lambda e, _, dst=dst, k=k: e.activation(dst[:, :], column(6)[:, k:k + 2], ACT.Copy), s_act0)
        braw = [[column(2), column(3)], [column(4), column(5)]]
        bvraw = column(6)[:, 4:6]
        split = [put_split(WH[:, :, col:col + D], WL[:, :, col:col + D], rQKV[:, :, col:col + D], load_q) for col in (COL_K, COL_Q, COL_V)]
        for w in (1, 0):
            pe.wait(split[1 - w])
            for b in range(DB):
                parts_block(w, b)
        pe.wait(split[2])
        values(0)
        pe.wait(cleared)
        i, m = product(P, [ones1], [alpha1], 1)
        dve.wait(m)
        alpha_in = dve.do(lambda e, _, i=i: e.tensor_copy(alphac, PS[:, i, 0:1]), s_dve0)
        bank[i].marks = [alpha_in]
        pe.wait(load_1)
        turned = []
        for src, dst in ((rWI, tWI), (rR1, tR1), (rWO, tWO)):
            for b in range(DB):
                i = next_bank()
                for a in range(DB):
                    m = pe.do(lambda e, _, a=a, b=b, i=i, src=src: e.transpose(PS[:, i, a * P:(a + 1) * P], src[:, a, b * P:(b + 1) * P], ident[:, :]), s_pe0)
                act.wait(m)
                turned.append(act.do(lambda e, _, b=b, i=i, dst=dst: e.activation(dst[:, b, :], PS[:, i, 0:D], ACT.Copy), s_act0))
                bank[i].marks = [turned[-1]]
        pe.wait(*turned)
        joined = []
        for src, dst in ((rWQ, gQ), (rWK, gK)):
            for f in range(DB):
                i, m = product(P, [tWI[:, e_, f * P:(f + 1) * P] for e_ in range(DB)], [src[:, e_, :] for e_ in range(DB)], D)
                act.wait(m)
                joined.append(act.do(lambda e, _, f=f, i=i, dst=dst: e.activation(dst[:, f, :], PS[:, i, 0:D], ACT.Copy), s_act0))
                bank[i].marks = [joined[-1]]
        act.wait(alpha_in)
        dve.wait(alpha_in)
        pe.wait(load_2)
        for left, right, col, n in ((rWQ, rV[0], COL_X, KR), (rWK, rV[2], COL_C, KR), (rWQ, tR1, COL_R, D), (gQ, tR1, COL_R + D, D),
                                    (gQ, rV[1], COL_X + KR, KR), (gK, rV[3], COL_C + KR, KR)):
            if left is gQ or left is gK:
                pe.wait(*joined)
            for d in range(DB):
                i, m = product(P, [left[:, e_, d * P:(d + 1) * P] for e_ in range(DB)], [right[:, e_, :] for e_ in range(DB)], n)
                bank[i].marks = [put_split(WH[:, d, col:col + n], WL[:, d, col:col + n], PS[:, i, 0:n], m)]
        pe.wait(load_3)
        put_split(OH[:, :, :], OL[:, :, :], rOUT, load_3)
        made = []
        for w in range(2):
            i, m = product(KE, braw[w], [tWO[:, e_, :] for e_ in range(DB)], D)
            dve.wait(m)
            made.append(dve.do(lambda e, _, i=i, w=w: e.tensor_scalar(brow[w], PS[0:KE, i, 0:D], alphac[0:KE, :] if w else 1.0, None, ALU.mult), s_dve0))
            bank[i].marks = [made[-1]]
        i, m = product(1, [bvraw[:, e_:e_ + 1] for e_ in range(DB)], [rOUT[:, e_, :] for e_ in range(DB)], D)
        dve.wait(m)
        made.append(dve.do(lambda e, _, i=i: e.tensor_tensor(brow[2], PS[0:1, i, 0:D], borow, ALU.add), s_dve0))
        bank[i].marks = [made[-1]]
        dve.wait(*made)
        for w in range(3):
            src = brow[w]
            for p in range(3):
                m = dve.do(lambda e, _, w=w, p=p, src=src: e.tensor_copy(bpart[w][p], src), s_dve0)
                dve.wait(m)
                if p < 2:
                    m2 = dve.do(lambda e, _, w=w, p=p, src=src: e.tensor_tensor(brest[w][p], src, bpart[w][p], ALU.subtract), s_dve0)
                    dve.wait(m2)
                    src = brest[w][p]
        last_pe, last_act, last_dve = (Mark(t_, t_.n) for t_ in (s_pe0, s_act0, s_dve0))
        act.wait(last_pe, made[-1])
        for q_ in (dve, pool, sp):
            q_.wait(last_pe, last_act, last_dve)
        pool.do(lambda e, _: e.memset(KG[G16:KSTK, :, :], 1.0), s_pool0)
        pool.do(lambda e, _: e.memset(KL[G16:KSTK, :, WINDOW:], 1.0), s_pool0)
        keep_keys(0)
        load_stacks(0, "local")
        load_stacks(0, "global")
        sp.wait(last_dve)
        for g in range(6):
            for w in range(2):
                sp.do(lambda e, _, g=g, w=w: e.dma_start(bias_rows[HD * g + KE * w:HD * g + KE * (w + 1), :], bpart[w][RIGHT[g]]), s_put0, 16)
        for p in range(3):
            put = sp.do(lambda e, _, p=p: e.dma_start(bias_rows[G16 + p:G16 + p + 1, :], bpart[2][p]), s_put0, 16)
        for j in range(2 * DB):
            hidden = router_hidden(0, j)
        act.wait(last_dve)
        router_logits(0, hidden)
        early = list(early_pairs)
        for w in range(2):
            for j in range(KB):
                i, m = product(P, [rU[w][:, e_, j * P:(j + 1) * P] for e_ in range(DB)], [tWO[:, e_, :] for e_ in range(DB)], D)
                bank[i].marks = [put_split(UH[:, KB * w + j, :], UL[:, KB * w + j, :], PS[:, i, 0:D], m,
                                           scale=alphac if w else None)]
                if KB * w + j >= 3:
                    for t, pair in early[:2]:
                        peaks_local(0, t, pair)
                    del early[:2]
        for t, pair in early:
            peaks_local(0, t, pair)
        sp.wait(put)
        for n in ("local_in", "global_in", "v_shift"):
            sp.wait_latest(now[n])
        setup = (pe, act, dve, pool, sp)
        pe, act, dve, pool, sp = (Queue() for _ in range(5))
        s = {n: tally(n) for n in names.split()}
        for thing in [*bank, *now.values(), *rest_slot, *he_slot, *prod_slot, *phl_slot, *craw_slot]:
            thing.marks = []

        def router_weights(c):
            pe.wait_latest(now["logits"])
            pe.wait_latest(bank[7])
            for t in range(T):
                m = pe.do(lambda e, _, t=t: e.transpose(psum(7, lo=t * P, hi=(t + 1) * P), logit_f[:, t * P:(t + 1) * P],
                                                        ident[:, :]), s["gate_t"])
            craw_slot[0].marks = [m]
            lg = psum(7).rearrange("p (t w a k) -> p t w a k", t=T, w=2, a=2)[:, :, :, :, 0:KE]
            g4 = [gate[:, k, :, :].rearrange("p t (w k) -> p (t w) k", k=KE) for k in range(4)]
            g5 = [gate[:, k, :, :].rearrange("p t (w k) -> p t w k", k=KE) for k in range(4)]
            dve.wait(m)
            dve.wait_latest(now["gate"])
            dve.wait(dve.do(lambda e, _: e.tensor_copy(g5[0], lg[:, :, :, 0, :]), s["gate_max"]))
            m = dve.do(lambda e, _: e.tensor_tensor(g5[3], lg[:, :, :, 1, :], g5[0], ALU.add), s["gate_max"])
            bank[7].marks = [m]
            dve.wait(m)
            dve.wait(dve.do(lambda e, _: e.tensor_reduce(gsum[:, 0, :], g4[3], AX_X, ALU.max), s["gate_max"]))
            m = dve.do(lambda e, _: e.tensor_tensor(g4[0], g4[3], gsum[:, 0, :].unsqueeze(2).to_broadcast([P, 2 * T, KE]), ALU.subtract), s["gate_max"])
            act.wait(m)
            m = act.do(lambda e, _: e.activation(g4[1], g4[0], ACT.Exp), s["gate_exp"])

            def finish_weights():
                dve.wait(m)
                router_parts(c, g4)
            return finish_weights

        def router_parts(c, g4):
            dve.wait(dve.do(lambda e, _: e.tensor_reduce(gsum[:, 1, :], g4[1], AX_X, ALU.add), s["gates"]))
            dve.wait(dve.do(lambda e, _: e.reciprocal(gsum[:, 2, :], gsum[:, 1, :]), s["gates"]))
            dve.wait(dve.do(lambda e, _: e.tensor_tensor(
                gsum[:, 3, :].rearrange("p (t w) -> p t w", w=2), gsum[:, 2, :].rearrange("p (t w) -> p t w", w=2),
                inv_n[:, c * T:(c + 1) * T].unsqueeze(2).to_broadcast([P, T, 2]), ALU.mult), s["gates"]))
            dve.wait(dve.do(lambda e, _: e.tensor_tensor(g4[2], g4[1], gsum[:, 3, :].unsqueeze(2).to_broadcast([P, 2 * T, KE]), ALU.mult), s["gates"]))
            dve.wait_latest(now["wstack"])
            ws = wstack[:, :, 0:G16].rearrange("p t (g k) -> p t g k", k=2 * KE)
            w_f, w_r = gate[:, 2], gate[:, 3]

            def copies(src, n):
                return src.unsqueeze(2).to_broadcast([P, T, n, 2 * KE])

            dve.wait(dve.do(lambda e, _: e.tensor_copy(ws[:, :, 0:3, :], copies(w_f, 3)), s["gates"]))
            dve.wait(dve.do(lambda e, _: e.tensor_tensor(w_r, w_f, ws[:, :, 0, :], ALU.subtract), s["gates"]))
            dve.wait(dve.do(lambda e, _: e.tensor_copy(ws[:, :, 3:5, :], copies(w_r, 2)), s["gates"]))
            m = dve.do(lambda e, _: e.tensor_tensor(ws[:, :, 5, :], w_r, ws[:, :, 3, :], ALU.subtract), s["gates"])
            now["gate"].marks = [m]
            return m

        def router_rows(c):
            pe.wait_latest(now["gate"])
            pe.wait_latest(bank[7])
            wt_ps = PS[0:KSTK, 7, :].bitcast(BF16)
            for t in range(T):
                m = pe.do(lambda e, _, t=t: e.transpose(wt_ps[:, t * P:(t + 1) * P], wstack[:, t, :], ident_b[:, :]), s["wt_t"])
            now["wstack"].marks = [m]
            act.wait(m)
            act.wait_latest(now["wt"])
            m = act.do(lambda e, _: e.activation(WT[:, :], wt_ps[:, 0:C], ACT.Copy), s["wt_in"])
            bank[7].marks = [m]
            now["rows"].marks = [m]

        def out_ps(t):
            return psum(t // 2, lo=(t % 2) * D, hi=(t % 2 + 1) * D)

        def open_out(c):
            pe.wait_latest(now["rows"])
            for t in range(T):
                if t % 2 == 0:
                    pe.wait_latest(bank[t // 2])
                pe.do(lambda e, _, t=t: e.matmul(out_ps(t), WT[:, t * P:(t + 1) * P], bias_rows[:, :], start=(t % 2 == 0), stop=False,
                                                 skip_group_check=True))

        halves = {}

        def expert_x(c, j, midway=None):
            r = j % 3
            pe.wait_latest(now["x"])
            m_x = project(2, COL_X + j * P, XH, XL, s["xv_ps"], midway)
            act.wait(m_x)
            act.wait_latest(prod_slot[r])
            m = act.do(lambda e, _: e.activation(prod[:, r, :], psum(2), ACT.Copy), s["xv_in"])
            bank[2].marks = [m]
            halves["x", j] = m
            if j == 2 * KB - 1:
                now["x_free"].marks = [m_x]

        def expert_c(c, j, midway=None):
            pe.wait_latest(now["c"])
            m_c = halves["c", j] = project(3, COL_C + j * P, CH, CL, s["cum_ps"], midway)
            if j == 2 * KB - 1:
                now["c_free"].marks = [m_c]

        def expert_product(c, j):
            r, h = j % 3, j % 2
            pe.wait_latest(now["rows"])
            pe.wait_latest(bank[4])
            m_w = pe.do(lambda e, _: e.matmul(psum(4), spread[:, j, :], WT[:, :], start=True, stop=True), s["w_ps"])
            dve.wait(halves["x", j], m_w)
            m = dve.do(lambda e, _: e.tensor_tensor(prod[:, r, :], psum(4), prod[:, r, :], ALU.mult), s["xvw"])
            bank[4].marks = [m]
            dve.wait(m, halves["c", j])
            m = dve.do(lambda e, _: e.tensor_tensor(prod[:, r, :], psum(3), prod[:, r, :], ALU.mult), s["xvwc"])
            bank[3].marks = [m]
            act.wait(m)
            act.wait_latest(phl_slot[h])
            mh = act.do(lambda e, _: e.activation(PH[:, h, :], prod[:, r, :], ACT.Copy), s["phi"])
            pool.wait(mh)
            ml = pool.do(lambda e, _: e.tensor_tensor(PL[:, h, :], prod[:, r, :], PH[:, h, :].bitcast(F32), ALU.subtract), s["plo"])
            prod_slot[r].marks = [ml]
            halves["p", j] = (mh, ml)
            if j == 2 * KB - 1:
                now["wt"].marks = [m_w]

        def mix(c, j, midway=None):
            h = j % 2
            mh, ml = halves["p", j]
            pe.wait(mh)
            for part, uu in ((PH, (UH, UL)), (PL, (UH,))):
                if part is PL:
                    if midway:
                        midway()
                    pe.wait(ml)
                for t in range(T):
                    for u in uu:
                        m = pe.do(lambda e, _, t=t, part=part, u=u: e.matmul(
                            out_ps(t), part[:, h, t * P:(t + 1) * P], u[:, j, :], start=False, stop=False, skip_group_check=True), s["mixed"])
            phl_slot[h].marks = [m]

        def peaks_global(c, t, g):
            start = LOWEST
            if t == 0 and g == 0:
                pe.wait_latest(now["global_in"])
                dve.wait_latest(now["peak1"])
            for q in range(c + 1):
                i = score_bank()
                n = C if q < c else (t + 1) * P
                pe.wait_latest(bank[i])
                m = pe.do(lambda e, _, q=q, n=n, i=i: e.matmul(psum(i, hi=n), QS[0:G16, g, t * P:(t + 1) * P], KG[0:G16, g, q * C:q * C + n],
                                                               start=True, stop=True), s["scores"])
                dve.wait(m)
                if q < c:
                    m = dve.do(lambda e, _, i=i: e.tensor_reduce(peak_part[:, t, g:g + 1], psum(i), AX_X, ALU.max), s["peak_parts"])
                    bank[i].marks = [m]
                    dve.wait(m)
                    start = peak_part[:, t, g:g + 1]
                else:
                    m = dve.do(lambda e, _, n=n, i=i, start=start: e.tensor_tensor_reduce(
                        psum(i, hi=n), psum(i, hi=n), strip[:, C - n:C], 1.0, start, ALU.add, ALU.max, peak[:, t, g:g + 1]), s["peaks"], apart=True)
                    bank[i].marks = [m]
            return m

        def peaks_to_rows(c, kind, found):
            lo, n = ((NG, NL), (0, NG))[kind]
            values_, left = peak[:, :, lo:lo + n], peak_rest[:, :, lo:lo + n]
            pt = [peak_t[kind][:, :, k * n:(k + 1) * n] for k in range(3)]
            dve.wait(found)
            dve.wait_latest(now[f"peak_t{kind}"])
            dve.wait(dve.do(lambda e, _: e.tensor_scalar(pt[0], values_, -1.0, None, ALU.mult), s["peak_parts"]))
            dve.wait(dve.do(lambda e, _: e.scalar_tensor_tensor(out=left, in0=values_, scalar=-1.0, in1=pt[0],
                                                                op0=ALU.mult, op1=ALU.subtract), s["peak_parts"]))
            dve.wait(dve.do(lambda e, _: e.tensor_copy(pt[1], left), s["peak_parts"]))
            m = dve.do(lambda e, _: e.tensor_tensor(pt[2], left, pt[1], ALU.subtract), s["peak_parts"])
            now[f"peak{kind}"].marks = [m]

            def turn():
                pe.wait(m)
                pe.wait_latest(bank[4])
                ps = PS[0:3 * n, 4, :].bitcast(BF16)
                for t in range(T):
                    m2 = pe.do(lambda e, _, t=t: e.transpose(ps[:, t * P:(t + 1) * P], peak_t[kind][:, t, :], ident_b[:, :]), s["peak_turned"], apart=(t == 0))
                now[f"peak_t{kind}"].marks = [m2]
                act.wait(m2)
                act.wait_latest(now["peak_f"])
                m2 = act.do(lambda e, _: e.activation(peak_f[0:3 * n, :], ps[:, 0:C], ACT.Copy), s["peak_copied"])
                bank[4].marks = [m2]
                sp.wait(m2)
                sp.wait_latest(now[f"peak_d{kind}"])
                m2 = sp.do(lambda e, _: e.dma_start(peak_d[kind], peak_f[0:3 * n, :]), s[f"peak_out{kind}"], 16)
                now["peak_f"].marks = [m2]
                sp.wait(m2)
                m2 = sp.do(lambda e, _: e.dma_start(QS[G16:KSTK, lo:lo + n, :], peak_d[kind].rearrange("(a h) t -> a h t", h=n)), s[f"peak_in{kind}"], 16)
                now[f"peak_d{kind}"].marks = [m2]
            return turn

        def exp_slot():
            turns["exp"] = (turns["exp"] + 1) % 4
            return turns["exp"]

        def attend_local(c, grp, half, pair, slots, ready):
            i, k = score_bank(), exp_slot()
            slots.append(k)
            pe.wait_latest(bank[i])
            pe.do(lambda e, _, i=i: e.matmul(psum(i).rearrange("p (w q) -> p w q", w=8), ident_b[:, :],
                                             mask_l[:, :].unsqueeze(1).to_broadcast([P, 8, WINDOW]),
                                             start=True, stop=False, skip_group_check=True))
            pe.wait_latest(now["peak_d0"])
            for a in range(2):
                l = 4 * (grp - 1) + 2 * pair + a
                for w in range(4):
                    at_ = (4 * half + w) * WINDOW
                    m = pe.do(lambda e, _, a=a, l=l, w=w, at_=at_, i=i: e.matmul(
                        psum(i, lo=(4 * a + w) * WINDOW, hi=(4 * a + w + 1) * WINDOW), KL[0:KSTK, l, at_:at_ + P],
                        QS[0:KSTK, NG + l, at_:at_ + WINDOW], start=False, stop=(a == 1 and w == 3), skip_group_check=True), s["st"])
            act.wait(m)
            act.wait_latest(he_slot[k])
            m = act.do(lambda e, _, i=i, k=k: e.activation(HE[:, k, :], psum(i), ACT.Exp, scale=SCALE), s["exped"])
            bank[i].marks = [m]
            ready.append(m)

        def local_products(c, grp, half, slots, ready):
            cb = 7
            if grp == 1 and half == 0:
                pe.wait_latest(now["v"])
                pe.wait_latest(now["v_shift"])
            pe.wait(*ready)
            if half == 0:
                pe.wait_latest(bank[cb])
            for w in range(4):
                for g in range(4):
                    l = 4 * (grp - 1) + g
                    t_, odd = c * T + 2 * half + w // 2, w % 2
                    v = Va[:, t_, NG + l, :] if odd else Vs[:, 2 * half + w // 2, l, :]
                    q = slice((4 * half + w) * WINDOW, (4 * half + w + 1) * WINDOW)
                    e_at = slice((4 * (g % 2) + w) * WINDOW, (4 * (g % 2) + w + 1) * WINDOW)
                    m2 = pe.do(lambda e, _, v=v, q=q, g=g, e_at=e_at, first=(half == 0 and w == 0): e.matmul(
                        PS[32 * g:32 * g + VW, cb, q], v, HE[:, slots[g // 2], e_at], start=first, stop=True,
                        skip_group_check=True), s["av"])
            for k in slots:
                he_slot[k].marks = [m2]
            return m2, cb

        def attend_global(c, j, half):
            HALF = C // 2
            lo = max(0, (j - c * T) * P - half * HALF)
            q = slice(half * HALF + lo, (half + 1) * HALF)
            diag = (j - c * T) * P >= half * HALF
            slots, ready = [], []
            for pair in range(2):
                i, k = score_bank(), exp_slot()
                slots.append(k)
                two = lambda ap: ap.rearrange("p (a q) -> p a q", a=2)[:, :, lo:]
                pe.wait_latest(bank[i])
                if diag:
                    pe.do(lambda e, _, i=i: e.matmul(two(psum(i))[:, :, 0:P], ident_b[:, :], mask_g[:, :].unsqueeze(1).to_broadcast([P, 2, P]),
                                                     start=True, stop=False, skip_group_check=True))
                pe.wait_latest(now["peak_d1"])
                for a in range(2):
                    g = 2 * pair + a
                    m = pe.do(lambda e, _, a=a, g=g, i=i: e.matmul(psum(i, lo=HALF * a + lo, hi=HALF * (a + 1)), KG[0:KSTK, g, j * P:(j + 1) * P],
                                                                   QS[0:KSTK, g, q], start=(a == 0 and not diag), stop=(a == 1), skip_group_check=True), s["st"])
                act.wait(m)
                act.wait_latest(he_slot[k])
                m = act.do(lambda e, _, i=i, k=k: e.activation(two(HE[:, k, :]), two(psum(i)), ACT.Exp, scale=SCALE), s["exped"])
                bank[i].marks = [m]
                ready.append(m)
            last = (j - c * T + 1) * P >= (half + 1) * HALF

            def av():
                pe.wait(*ready)
                if j == 0 and half == 0:
                    pe.wait_latest(bank[4])
                for g in range(4):
                    e_at = slice(HALF * (g % 2) + lo, HALF * (g % 2 + 1))
                    m2 = pe.do(lambda e, _, g=g, e_at=e_at: e.matmul(PS[32 * g:32 * g + VW, 4, q], Va[:, j, g, :], HE[:, slots[g // 2], e_at],
                                                                     start=(j == 0 and half == 0), stop=last, skip_group_check=True), s["av"])
                for k in slots:
                    he_slot[k].marks = [m2]
                return m2, 4
            return av

        def context_in(c, grp, done):
            m, cb = done
            r = grp % 2
            act.wait(m)
            act.wait_latest(craw_slot[r])
            m = act.do(lambda e, _: e.activation(craw[:, r, :], psum(cb), ACT.Copy), s["craw_in"])
            bank[cb].marks = [m]
            return m

        def context_out(c, grp, m):
            r = grp % 2
            tb = 4 if grp in (1, 2) else 2 + r
            pe.wait(m)
            pe.wait_latest(bank[tb])
            for t in range(T):
                m = pe.do(lambda e, _, t=t: e.transpose(psum(tb, lo=t * P, hi=(t + 1) * P), craw[:, r, t * P:(t + 1) * P], ident[:, :]), s["ctx_t"])
            craw_slot[r].marks = [m]
            raw_t = psum(tb).rearrange("p (t g e) -> p t g e", t=T, g=4)
            dve.wait(m)
            if grp == 1:
                dve.wait_latest(now["ctok"])
            dve.wait(dve.do(lambda e, _: e.reciprocal(cinv[:, r, :, :], raw_t[:, :, :, HD]), s["ctx_rec"]))
            m = dve.do(lambda e, _: e.tensor_tensor(
                ctok[:, :, grp * 64:(grp + 1) * 64].rearrange("p t (g d) -> p t g d", g=4), raw_t[:, :, :, 0:HD],
                cinv[:, r, :, :].unsqueeze(3).to_broadcast([P, T, 4, HD]), ALU.mult), s["ctx_tok"])
            bank[tb].marks = [m]
            return m

        def context_parts(c, ready):
            pe.wait(ready)
            marks = []
            for k in range(DB):
                i = 2 + k
                pe.wait_latest(bank[i])
                for t in range(T):
                    m = pe.do(lambda e, _, t=t, k=k, i=i: e.transpose(psum(i, lo=t * P, hi=(t + 1) * P), ctok[:, t, k * P:(k + 1) * P], ident[:, :]), s["ctx_f"])
                act.wait(m)
                act.wait_latest(phl_slot[k])
                mh = act.do(lambda e, _, k=k, i=i: e.activation(PH[:, k, :], psum(i), ACT.Copy), s["ctx_hi"])
                dve.wait(mh)
                ml = dve.do(lambda e, _, k=k, i=i: e.tensor_tensor(PL[:, k, :], psum(i), PH[:, k, :].bitcast(F32), ALU.subtract), s["ctx_lo"])
                bank[i].marks = [ml]
                marks += [mh, ml]
            now["ctok"].marks = [m]
            return marks

        def finish(c, marks):
            pe.wait(*marks)
            X = xt[c]
            for u in range(T // 2):
                for t in (2 * u, 2 * u + 1):
                    for k in range(DB):
                        for a, b in ((PH, OH), (PH, OL), (PL, OH)):
                            m = pe.do(lambda e, _, t=t, k=k, a=a, b=b: e.matmul(
                                out_ps(t), a[:, k, t * P:(t + 1) * P], b[:, k, :], start=False,
                                stop=(k == DB - 1 and a is PL), skip_group_check=True), s["out_ps"])
                dve.wait(m)
                my = dve.do(lambda e, _, u=u: e.tensor_tensor(X[:, 2 * u:2 * u + 2, :], psum(u).rearrange("p (a d) -> p a d", a=2),
                                                              X[:, 2 * u:2 * u + 2, :], ALU.add), s["y"])
                bank[u].marks = [my]
            for h in range(2):
                phl_slot[h].marks = [m]
            sp.wait(my)
            mo = sp.do(lambda e, n: e.dma_start(outr[n, c], X[:, :, :]), s[f"stored{c}"], 16, apart=True)
            now[f"xt{c}"].marks = [mo]

        for c in range(NC):
            nxt = (c + 1) % NC
            load_x(nxt, (lambda n: n) if nxt else (lambda n: (n + 1) % NB))
            found, late, contexts, steps = [], [], [], {}

            def flush(keep):
                while contexts:
                    found.append(context_out(c, *contexts.pop(0)))
                while len(late) > keep:
                    grp, av, closes = late.pop(0)
                    done = av()
                    if closes:
                        contexts.append((grp, context_in(c, grp, done)))

            def peak_unit(f, t, a):
                def run():
                    steps["found"] = f(c, t, a)
                return run

            def both(a, b):
                return lambda: (a(), b())

            def find_rows(kind):
                def run():
                    steps["turn", kind] = peaks_to_rows(c, kind, steps["found"])
                return run

            def turn_rows(kind):
                return lambda: steps["turn", kind]()

            def local_units(grp, half):
                slots, ready = [], []

                def products():
                    late.append((grp, lambda: local_products(c, grp, half, slots, ready), half == 1))
                    flush(1)
                return [lambda pair=pair: attend_local(c, grp, half, pair, slots, ready) for pair in range(2)] + [products]

            locals_ = [unit for grp in range(1, 1 + NL // 4) for half in range(2) for unit in local_units(grp, half)]
            norm = normalise(nxt)
            side = [peak_unit(peaks_local, t, p) for t, p in later_pairs] + [find_rows(0)]
            global_units = [peak_unit(peaks_global, t, g) for t in range(T) for g in range(NG)]
            for k, unit in enumerate(global_units):
                side.append(unit)
                if k == 0:
                    side.append(turn_rows(0))
                if k >= FIRST_LOCAL:
                    take = max(1, (len(locals_) - LAST_LOCALS) // (len(global_units) - k))
                    side += locals_[:take]
                    del locals_[:take]
                if k >= 2 and norm:
                    side.append(both(side.pop(), norm.pop(0)))
            side += locals_[:-LAST_LOCALS]
            del locals_[:-LAST_LOCALS]
            gone = [0, 0]

            def fill():
                gone[0] += 1
                upto = min(len(side), len(side) * gone[0] // FILLS)
                for unit in side[gone[1]:upto]:
                    unit()
                gone[1] = upto

            expert_x(c, 0)
            finish_weights = router_weights(c)
            fill()
            expert_c(c, 0, fill)
            finish_weights()
            fill()
            for j in range(8):
                if j < 7:
                    expert_x(c, j + 1, fill)
                    fill()
                if j:
                    expert_c(c, j, fill)
                else:
                    router_rows(c)
                fill()
                expert_product(c, j)
                if j:
                    mix(c, j - 1, fill)
                else:
                    open_out(c)
                fill()
            assert gone[1] == len(side) and not norm
            find_rows(1)()
            turn_tokens(nxt)
            for unit in locals_:
                unit()
            mix(c, 7)
            turn_rows(1)()
            parts_block(1, 0)
            parts_block(1, 1)
            parts_block(0, 0)
            parts_block(0, 1)
            now["local"].marks = [Mark(s["st"], s["st"].n)]
            tiles = [(j, half) for j in range((c + 1) * T) for half in range(2) if (half + 1) * (C // 2) > (j - c * T) * P]
            for k, (j, half) in enumerate(tiles):
                late.append((0, attend_global(c, j, half), (j, half) == tiles[-1]))
                flush(1)
                if k == 0:
                    keep_keys(nxt)
                    load_stacks(nxt, "local")
            now["global"].marks = [Mark(s["st"], s["st"].n)]
            load_stacks(nxt, "global")
            flush(0)
            now["va"].marks = [Mark(s["av"], s["av"].n)] + (now["v_shift"].marks if c else [])
            now["vs"].marks = [Mark(s["av"], s["av"].n)]
            early = [(lambda t=t, p=p: peaks_local(nxt, t, p)) for t, p in early_pairs]

            def early_peaks(n):
                for unit in early[:n]:
                    unit()
                del early[:n]

            values(nxt)
            flush(0)
            router_hidden(nxt, 0)
            early_peaks(2)
            router_hidden(nxt, 1)
            early_peaks(1)
            marks = context_parts(c, found[-1])
            router_hidden(nxt, 2)
            early_peaks(2)
            hidden = router_hidden(nxt, 3)
            early_peaks(2)
            finish(c, marks)
            early_peaks(1)
            router_logits(nxt, hidden)
            early_peaks(len(early))

        with nc.Block() as block:
            block.tensor(lambda e: setup[0].write(e))
            block.scalar(lambda e: setup[1].write(e))
            block.vector(lambda e: setup[2].write(e))
            block.gpsimd(lambda e: setup[3].write(e))
            block.sync(lambda e: setup[4].write(e))

        body = (pe, act, dve, pool, sp)

        def looped(queue):
            def program(e):
                with e.Fori(0, NB) as n:
                    queue.write(e, n, waits_apart=queue is sp)
                if queue is sp:
                    for name in ("stored0", "stored1", "local_in", "global_in", "vs_in"):
                        e.wait_ge(s[name].sem, s[name].n * (NB + 1))
            return program

        with nc.Block() as block:
            block.tensor(looped(body[0]))
            block.scalar(looped(body[1]))
            block.vector(looped(body[2]))
            block.gpsimd(looped(body[3]))
            block.sync(looped(body[4]))


_INS = ['L0_attn_x', 'L0_attn_w_qkv', 'L0_attn_b_qkv', 'L0_attn_w_out', 'L0_attn_b_out', 'L0_ffn_W_Q', 'L0_ffn_W_K',
        'L0_ffn_W_O', 'L0_ffn_W_inv', 'L0_ffn_V_fwd', 'L0_ffn_W_fwd', 'L0_ffn_U_fwd', 'L0_ffn_b_fwd', 'L0_ffn_V_inv',
        'L0_ffn_W_inv_exp', 'L0_ffn_U_inv', 'L0_ffn_b_inv', 'L0_ffn_router_w1', 'L0_ffn_router_b1', 'L0_ffn_router_w2',
        'L0_ffn_router_b2', 'L0_ffn_alpha_bi', 'L0_ffn_expert_bias']


def kernel(**inputs):
    import numpy as _np
    import concourse.bacc as _bacc
    from concourse import mybir as _mybir
    from concourse.bass_utils import run_bass_kernel_spmd as _run

    nc = _bacc.Bacc("TRN2", target_bir_lowering=False, num_devices=1)
    arrays, args = {}, []
    for name in _INS:
        a = _np.ascontiguousarray(inputs[name])
        if a.ndim == 0:
            a = a.reshape(1)
        arrays[f"in_{name}_dram"] = a
        args.append(nc.dram_tensor(f"in_{name}_dram", a.shape, _mybir.dt.from_np(a.dtype), kind="ExternalInput").ap())
    shape = tuple(inputs['L0_attn_x'].shape)
    args.append(nc.dram_tensor("out_0_dram", shape, _mybir.dt.float32, kind="ExternalOutput").ap())
    with nc.allow_non_contiguous_dma("small weights are read by columns once"):
        mixer_layer(nc, *args)
    r = _run(nc, [arrays], core_ids=[0])
    return r.results[0]["out_0_dram"]
```
